# Optimizing a Trainium2 kernel written in Bass

```python
import numpy as np
import jax
import jax.numpy as jnp

def _softmax(x, axis=-1):
    return jax.nn.softmax(x, axis=axis)

def _gelu(x):
    return jax.nn.gelu(x, approximate=True)

def _silu(x):
    return jax.nn.silu(x)

def _sigmoid(x):
    return jax.nn.sigmoid(x)

def _layernorm(x, axis=-1, eps=1e-05):
    m = jnp.mean(x, axis=axis, keepdims=True)
    v = jnp.var(x, axis=axis, keepdims=True)
    return (x - m) / jnp.sqrt(v + eps)

def _scatter_add(tgt, idx, src, axis=0):
    return tgt.at[idx].add(src)

def _segment_sum(src, seg, n):
    return jax.ops.segment_sum(src, seg, n)
kernel_name = 'mk_sandwich_d1_jaxref_r8_877b7d'

def setup_inputs(seed: int=0):
    np.random.seed(seed)
    _w = jnp.asarray

    def _L0_attn_setup():
        import jax, jax.numpy as jnp
        import numpy as np
        B, S, D = (8, 256, 128)
        key = jax.random.key(seed)
        k1, k2, k3, k4 = jax.random.split(key, 4)
        x = jax.random.normal(k1, (B, S, D), dtype=jnp.float32)
        W0 = jax.random.normal(k2, (D, D), dtype=jnp.float32) / jnp.sqrt(jnp.float32(D))
        Wkv = jax.random.normal(k3, (2 * D, D), dtype=jnp.float32) / jnp.sqrt(jnp.float32(D))
        bkv = jax.random.normal(k4, (2 * D,), dtype=jnp.float32) * 0.01
        eta = jnp.float32(0.1)
        return {'x': x, 'W0': W0, 'Wkv': Wkv, 'bkv': bkv, 'eta': eta}
    _L0_attn_in = _L0_attn_setup()

    def _L0_ffn_setup():
        import jax, jax.numpy as jnp
        import numpy as np
        DIM = 128
        DEPTH = 6
        HEADS = 16
        DIM_HEAD = 64
        WINDOW = 32
        INNER = HEADS * DIM_HEAD
        DIM_INNER = int(DIM * 4 * 2 / 3)
        QK_SCALE = 8.0

        def shift_tokens(t):
            a, s = jnp.split(t, 2, -1)
            s = jnp.pad(s, ((0, 0), (1, 0), (0, 0)))[:, :-1]
            return jnp.concatenate([a, s], -1)

        def l2norm(t):
            return t / jnp.maximum(jnp.linalg.norm(t, axis=-1, keepdims=True), 1e-12)

        def rotate_half(x):
            x1, x2 = jnp.split(x, 2, -1)
            return jnp.concatenate([-x2, x1], -1)

        def rotary_tables(n):
            half = jnp.arange(0, DIM_HEAD, 2, dtype=jnp.float32)
            inv_freq = 1.0 / 10000.0 ** (half / DIM_HEAD)
            t = jnp.arange(n, dtype=jnp.float32)
            freqs = t[:, None] * inv_freq[None, :]
            freqs = jnp.concatenate([freqs, freqs], -1)
            base_scale = (half + 0.4 * DIM_HEAD) / (1.4 * DIM_HEAD)
            power = (t - n // 2) / (WINDOW // 2)
            scale = base_scale[None, :] ** power[:, None]
            scale = jnp.concatenate([scale, scale], -1)
            return (freqs, scale)

        def local_attention(q, k, v):
            b, h, n, d = q.shape
            w = WINDOW
            nw = n // w
            bq = q.reshape(b, h, nw, w, d)
            bk = k.reshape(b, h, nw, w, d)
            bv = v.reshape(b, h, nw, w, d)

            def look(t):
                p = jnp.pad(t, ((0, 0), (0, 0), (1, 0), (0, 0), (0, 0)))
                return jnp.concatenate([p[:, :, :nw], p[:, :, 1:]], axis=3)
            bk2, bv2 = (look(bk), look(bv))
            seq = jnp.arange(n).reshape(nw, w)
            seq_p = jnp.pad(seq, ((1, 0), (0, 0)), constant_values=-1)
            jt = jnp.concatenate([seq_p[:nw], seq_p[1:]], axis=1)
            it = seq[:, :, None]
            jb = jt[:, None, :]
            mask = (it < jb) | (it > jb + w) | (jb == -1)
            sim = jnp.einsum('bhwie,bhwje->bhwij', bq, bk2) * QK_SCALE
            sim = jnp.where(mask, -jnp.finfo(sim.dtype).max, sim)
            attn = jax.nn.softmax(sim, -1)
            out = jnp.einsum('bhwij,bhwje->bhwie', attn, bv2)
            return out.reshape(b, h, n, d)

        def attn_layer(x, Wqkv, qs, ksc, Wo):
            b, n, _ = x.shape
            qkv = x @ Wqkv
            q, k, v = jnp.split(qkv, 3, -1)
            sh = lambda t: t.reshape(b, n, HEADS, DIM_HEAD).transpose(0, 2, 1, 3)
            q, k, v = (sh(q), sh(k), sh(v))
            q = l2norm(q) * qs
            k = l2norm(k) * ksc
            freqs, scale = rotary_tables(n)
            cos, sin = (jnp.cos(freqs), jnp.sin(freqs))
            q = q * cos * scale + rotate_half(q) * sin * scale
            inv = 1.0 / scale
            k = k * cos * inv + rotate_half(k) * sin * inv
            out = local_attention(q, k, v)
            out = out.transpose(0, 2, 1, 3).reshape(b, n, INNER)
            return out @ Wo

        def ffn_layer(x, g, bln, W1, b1, W2, b2):
            mu = x.mean(-1, keepdims=True)
            var = ((x - mu) ** 2).mean(-1, keepdims=True)
            xn = (x - mu) / jnp.sqrt(var + 1e-05) * g + bln
            hg = xn @ W1 + b1
            a, gate = jnp.split(hg, 2, -1)
            return a * jax.nn.gelu(gate, approximate=False) @ W2 + b2
        key = jax.random.key(seed)
        ks = jax.random.split(key, 8)
        B, N = (2, 256)
        init = lambda k, shape: jax.random.normal(k, shape, jnp.float32) * 0.02
        return {'x': jax.random.normal(ks[0], (B, N, DIM), jnp.float32), 'Wqkv': init(ks[1], (DEPTH, DIM, 3 * INNER)), 'q_scale': jnp.ones((DEPTH, DIM_HEAD), jnp.float32), 'k_scale': jnp.ones((DEPTH, DIM_HEAD), jnp.float32), 'Wo': init(ks[2], (DEPTH, INNER, DIM)), 'ln_g': jnp.ones((DEPTH, DIM), jnp.float32), 'ln_b': jnp.zeros((DEPTH, DIM), jnp.float32), 'W1': init(ks[3], (DEPTH, DIM, 2 * DIM_INNER)), 'b1': jnp.zeros((DEPTH, 2 * DIM_INNER), jnp.float32), 'W2': init(ks[4], (DEPTH, DIM_INNER, DIM)), 'b2': jnp.zeros((DEPTH, DIM), jnp.float32)}
    _L0_ffn_in = _L0_ffn_setup()
    _d = {'L0_attn_x': _L0_attn_in['x'], 'L0_attn_W0': _L0_attn_in['W0'], 'L0_attn_Wkv': _L0_attn_in['Wkv'], 'L0_attn_bkv': _L0_attn_in['bkv'], 'L0_attn_eta': _L0_attn_in['eta'], 'L0_ffn_Wqkv': _L0_ffn_in['Wqkv'], 'L0_ffn_q_scale': _L0_ffn_in['q_scale'], 'L0_ffn_k_scale': _L0_ffn_in['k_scale'], 'L0_ffn_Wo': _L0_ffn_in['Wo'], 'L0_ffn_ln_g': _L0_ffn_in['ln_g'], 'L0_ffn_ln_b': _L0_ffn_in['ln_b'], 'L0_ffn_W1': _L0_ffn_in['W1'], 'L0_ffn_b1': _L0_ffn_in['b1'], 'L0_ffn_W2': _L0_ffn_in['W2'], 'L0_ffn_b2': _L0_ffn_in['b2']}
    _x0 = _d['L0_attn_x']
    _d['L0_attn_x'] = jax.random.normal(jax.random.fold_in(jax.random.key(seed), 1), (1, 2048, 128), dtype=_x0.dtype)
    del _x0
    return _d

def reference(L0_attn_x, L0_attn_W0, L0_attn_Wkv, L0_attn_bkv, L0_attn_eta, L0_ffn_Wqkv, L0_ffn_q_scale, L0_ffn_k_scale, L0_ffn_Wo, L0_ffn_ln_g, L0_ffn_ln_b, L0_ffn_W1, L0_ffn_b1, L0_ffn_W2, L0_ffn_b2):

    def _L0_attn_ref(x, W0, Wkv, bkv, eta):
        import jax, jax.numpy as jnp
        import numpy as np
        B, S, D = (8, 256, 128)
        b, s, d = x.shape
        v = jnp.einsum('bsd,ed->bse', x, Wkv[d:, :]) + bkv[d:]
        scale = 2.0 / (b * d)

        def step(W, inp):
            xt, vt = inp
            y = xt @ W.T
            err = y - vt
            gW = scale * (err.T @ xt)
            return (W - eta * gW, y)
        xs = jnp.swapaxes(x, 0, 1)
        vs = jnp.swapaxes(v, 0, 1)
        _, ys = jax.lax.scan(step, W0, (xs, vs))
        return jnp.swapaxes(ys, 0, 1)

    def _L0_ffn_ref(x, Wqkv, q_scale, k_scale, Wo, ln_g, ln_b, W1, b1, W2, b2):
        import jax, jax.numpy as jnp
        import numpy as np
        DIM = 128
        DEPTH = 6
        HEADS = 16
        DIM_HEAD = 64
        WINDOW = 32
        INNER = HEADS * DIM_HEAD
        DIM_INNER = int(DIM * 4 * 2 / 3)
        QK_SCALE = 8.0

        def shift_tokens(t):
            a, s = jnp.split(t, 2, -1)
            s = jnp.pad(s, ((0, 0), (1, 0), (0, 0)))[:, :-1]
            return jnp.concatenate([a, s], -1)

        def l2norm(t):
            return t / jnp.maximum(jnp.linalg.norm(t, axis=-1, keepdims=True), 1e-12)

        def rotate_half(x):
            x1, x2 = jnp.split(x, 2, -1)
            return jnp.concatenate([-x2, x1], -1)

        def rotary_tables(n):
            half = jnp.arange(0, DIM_HEAD, 2, dtype=jnp.float32)
            inv_freq = 1.0 / 10000.0 ** (half / DIM_HEAD)
            t = jnp.arange(n, dtype=jnp.float32)
            freqs = t[:, None] * inv_freq[None, :]
            freqs = jnp.concatenate([freqs, freqs], -1)
            base_scale = (half + 0.4 * DIM_HEAD) / (1.4 * DIM_HEAD)
            power = (t - n // 2) / (WINDOW // 2)
            scale = base_scale[None, :] ** power[:, None]
            scale = jnp.concatenate([scale, scale], -1)
            return (freqs, scale)

        def local_attention(q, k, v):
            b, h, n, d = q.shape
            w = WINDOW
            nw = n // w
            bq = q.reshape(b, h, nw, w, d)
            bk = k.reshape(b, h, nw, w, d)
            bv = v.reshape(b, h, nw, w, d)

            def look(t):
                p = jnp.pad(t, ((0, 0), (0, 0), (1, 0), (0, 0), (0, 0)))
                return jnp.concatenate([p[:, :, :nw], p[:, :, 1:]], axis=3)
            bk2, bv2 = (look(bk), look(bv))
            seq = jnp.arange(n).reshape(nw, w)
            seq_p = jnp.pad(seq, ((1, 0), (0, 0)), constant_values=-1)
            jt = jnp.concatenate([seq_p[:nw], seq_p[1:]], axis=1)
            it = seq[:, :, None]
            jb = jt[:, None, :]
            mask = (it < jb) | (it > jb + w) | (jb == -1)
            sim = jnp.einsum('bhwie,bhwje->bhwij', bq, bk2) * QK_SCALE
            sim = jnp.where(mask, -jnp.finfo(sim.dtype).max, sim)
            attn = jax.nn.softmax(sim, -1)
            out = jnp.einsum('bhwij,bhwje->bhwie', attn, bv2)
            return out.reshape(b, h, n, d)

        def attn_layer(x, Wqkv, qs, ksc, Wo):
            b, n, _ = x.shape
            qkv = x @ Wqkv
            q, k, v = jnp.split(qkv, 3, -1)
            sh = lambda t: t.reshape(b, n, HEADS, DIM_HEAD).transpose(0, 2, 1, 3)
            q, k, v = (sh(q), sh(k), sh(v))
            q = l2norm(q) * qs
            k = l2norm(k) * ksc
            freqs, scale = rotary_tables(n)
            cos, sin = (jnp.cos(freqs), jnp.sin(freqs))
            q = q * cos * scale + rotate_half(q) * sin * scale
            inv = 1.0 / scale
            k = k * cos * inv + rotate_half(k) * sin * inv
            out = local_attention(q, k, v)
            out = out.transpose(0, 2, 1, 3).reshape(b, n, INNER)
            return out @ Wo

        def ffn_layer(x, g, bln, W1, b1, W2, b2):
            mu = x.mean(-1, keepdims=True)
            var = ((x - mu) ** 2).mean(-1, keepdims=True)
            xn = (x - mu) / jnp.sqrt(var + 1e-05) * g + bln
            hg = xn @ W1 + b1
            a, gate = jnp.split(hg, 2, -1)
            return a * jax.nn.gelu(gate, approximate=False) @ W2 + b2
        for i in range(DEPTH):
            x = attn_layer(shift_tokens(x), Wqkv[i], q_scale[i], k_scale[i], Wo[i]) + x
            x = ffn_layer(shift_tokens(x), ln_g[i], ln_b[i], W1[i], b1[i], W2[i], b2[i]) + x
        return x
    x = L0_attn_x
    x = x + _layernorm(_L0_attn_ref(_layernorm(x, axis=-1), L0_attn_W0, L0_attn_Wkv, L0_attn_bkv, L0_attn_eta), axis=-1)
    x = x + _layernorm(_L0_ffn_ref(_layernorm(x, axis=-1), L0_ffn_Wqkv, L0_ffn_q_scale, L0_ffn_k_scale, L0_ffn_Wo, L0_ffn_ln_g, L0_ffn_ln_b, L0_ffn_W1, L0_ffn_b1, L0_ffn_W2, L0_ffn_b2), axis=-1)
    return x

_drawn_inputs = setup_inputs


def setup_inputs(seed=0):
    import zlib

    import numpy as np

    out = dict(_drawn_inputs(seed))
    spreads = {'L0_ffn_q_scale': (1.0, 0.6),
     'L0_ffn_k_scale': (1.0, 0.6),
     'L0_ffn_ln_g': (1.0, 0.6),
     'L0_ffn_ln_b': (0.0, 0.8),
     'L0_ffn_b1': (0.0, 0.8),
     'L0_ffn_b2': (0.0, 0.334)}
    factors = {'L0_attn_bkv': 22.746, 'L0_ffn_W1': 4.528, 'L0_ffn_W2': 4.443}
    for name, (base, spread) in spreads.items():
        noise = np.random.default_rng([zlib.crc32(name.encode()), seed]).standard_normal(out[name].shape)
        drawn = base * np.exp(spread * noise) if base else spread * noise
        out[name] = jnp.asarray(drawn.astype(out[name].dtype))
    for name, factor in factors.items():
        out[name] = (out[name] * factor).astype(out[name].dtype)
    return out
```

```python
from contextlib import ExitStack

import concourse.bass as bass
from concourse import mybir

F32 = mybir.dt.float32
BF16 = mybir.dt.bfloat16
ALU = mybir.AluOpType
ACT = mybir.ActivationFunctionType
AX = mybir.AxisListType

P = 128
TOKENS = 2048
TILES = TOKENS // P
LAYERS = 6
QUAD = 4
GROUPS = TILES // QUAD
STEPS = LAYERS * TILES
HEADS, HD, WIN = 16, 64, 32
NWIN = P // WIN
KEYS = 2 * WIN
PAIRS = HEADS // 2
HID = 341
HBLK = [(0, 128), (128, 128), (256, HID - 256)]
PAD = 64
EPS = 1e-5
QK_SCALE = 8.0
LEVELS = 7


def head_of(a, g):
    return 2 * (4 * (a // 2) + g) + a % 2


def build(nc, x_d, wvT_d, w0T_d, bv_d, eta_d, wqk_d, scale_d, mvT_d, wo_d, w1_d, w2_d, par_d,
          ident_d, mask_d, rope_d, kfac_d, level_d, out_d):
    ctx = ExitStack()
    with ctx:
        def sb(name, shape, dt=F32):
            return ctx.enter_context(nc.sbuf_tensor(name, shape, dt))

        def sem(name):
            return ctx.enter_context(nc.semaphore(name))

        ident = sb("ident", [P, P])
        ident16 = sb("ident16", [P, P], BF16)
        mask16 = sb("mask16", [P, 2, 512], BF16)
        rope = sb("rope", [P, TILES, 4 * HD])
        kfac = sb("kfac", [P, 1])
        qk_scales = sb("qk_scales", [P, LAYERS, 4 * HD])
        wqk = sb("wqk", [P, LAYERS, 2 * HEADS * HD])
        neg_half = sb("neg_half", [P, 2 * HEADS])
        eps = sb("eps", [P, QUAD])
        eta_bc = sb("eta_bc", [P, 1])
        coef = sb("coef", [P, 2])
        x0 = sb("x0", [P, PAD + TOKENS])
        x1 = sb("x1", [P, PAD + TOKENS])
        xmid = sb("xmid", [P, TILES, P])
        mvT = sb("mvT", [P, PAIRS, P])
        wo = sb("wo", [P, PAIRS, P])
        mh = sb("mh", [P, HEADS, P])
        w1 = sb("w1", [P, 2 * HID])
        w2 = sb("w2", [P, 3, P])
        par = sb("par", [P, 9])
        xs = sb("xs", [P, 2, WIN + P])
        xw = sb("xw", [P, 4, 2, P])
        tab = sb("tab", [P, 4, HD])
        qa = sb("qa", [P, 2048])
        qb = sb("qb", [P, 2048])
        qn = sb("qn", [P, 2048])
        sq = qn
        ss = sb("ss", [P, 2 * HEADS])
        ssc = sb("ssc", [P, 2 * HEADS])
        rn = sb("rn", [P, 2 * HEADS])
        qT = sb("qT", [P, PAIRS, P])
        kT = sb("kT", [P, 2, PAIRS, 2, WIN + P])
        mx = sb("mx", [P, HEADS])
        den = sb("den", [P, HEADS])
        rden = sb("rden", [P, HEADS])
        pr = sb("pr", [P, 2, 1024])
        pT = sb("pT", [P, 2, 512])
        zT = sb("zT", [P, HEADS, NWIN, WIN])
        xs2 = sb("xs2", [P, 512])
        xf = sb("xf", [P, QUAD, P])
        xh = xf
        xnT = xs2
        bst = sb("bst", [P, QUAD, 6])
        mv = sb("mv", [P, QUAD, 2])
        vare = sb("vare", [P, QUAD])
        rstd = sb("rstd", [P, QUAD])
        gl = sb("gl", [P, 2, 512])
        uT = sb("uT", [P, 3, 512])
        kT_flat = kT[:, :, :, :, :].rearrange("p s a r n -> p (s a r n)")
        c_xn, c_xT, c_g, c_v = (kT_flat[:, 512 * i:512 * i + 512].rearrange("p (c n) -> p c n", c=4) for i in range(4))
        c_m, c_mT, c_q, c_u = (qn[:, 512 * i:512 * i + 512].rearrange("p (c n) -> p c n", c=4) for i in range(4))
        c_b = [(qa, qb)[i // 4][:, 512 * (i % 4):512 * (i % 4) + 512].rearrange("p (c n) -> p c n", c=4)
               for i in range(LEVELS - 1)]
        c_pT, c_qp = (pr[:, 0, 512 * i:512 * i + 512].rearrange("p (c n) -> p c n", c=4) for i in range(2))
        c_y, c_t = (pr[:, 1, 512 * i:512 * i + 512].rearrange("p (c n) -> p c n", c=4) for i in range(2))
        wT = uT[:, 0, 0:P]
        wvT = uT[:, 0, P:2 * P]
        bv = uT[:, 0, 2 * P:3 * P]
        level = mh[:, 0:LEVELS + 1, :]
        mask_in = zT[:, 0:8, :, :].rearrange("p h w i -> p (h w i)").rearrange("p (v n) -> p v n", v=2)

        psq = ctx.enter_context(nc.psum_tensor("psq", [P, 2048], F32))
        pt = [ctx.enter_context(nc.psum_tensor(f"pt{i}", [P, 512], F32)) for i in range(2)]
        pss = ctx.enter_context(nc.psum_tensor("pss", [P, 1024], F32))
        pbank = [psq[:, 512 * i:512 * i + 512].rearrange("p (c n) -> p c n", c=4) for i in range(4)]

        s_const = sem("s_const")
        s_wqk = sem("s_wqk")
        s_cv = sem("s_cv")
        s_lmask = sem("s_lmask")
        ve = sem("ve")
        pe1 = sem("pe1")
        pl1 = sem("pl1")
        s_kz = sem("s_kz")
        x0_first = sem("x0_first")
        xs_ready = [sem(f"xs_ready{k}") for k in range(2)]
        x_ready, x_copied = sem("x_ready"), sem("x_copied")
        proj_done = sem("proj_done")
        sq_done, ss_ready, ssc_ready, r_ready = sem("sq_done"), sem("ss_ready"), sem("ssc_ready"), sem("r_ready")
        tab_ready, rope_ab, rope_sum, qn_ready = sem("tab_ready"), sem("rope_ab"), sem("rope_sum"), sem("qn_ready")
        qkT_ready, qkT_copied, kprev_ready = sem("qkT_ready"), sem("qkT_copied"), sem("kprev_ready")
        s_ready, mx_ready, p_shifted, exp_done = sem("s_ready"), sem("mx_ready"), sem("p_shifted"), sem("exp_done")
        den_ready, rden_ready, p_ready = sem("den_ready"), sem("rden_ready"), sem("p_ready")
        pT_ready, pT_copied = sem("pT_ready"), sem("pT_copied")
        zT_ready, zT_copied = sem("zT_ready"), sem("zT_copied")
        y_ready, y_added = sem("y_ready"), sem("y_added")
        mw_ready, m_ready, m_copied = sem("mw_ready"), sem("m_ready"), sem("m_copied")
        fw_ready = sem("fw_ready")
        xs2_ready, xf_ready, xf_copied = sem("xs2_ready"), sem("xf_ready"), sem("xf_copied")
        bst_ready, mv_ready, vare_ready, rstd_ready = sem("bst_ready"), sem("mv_ready"), sem("vare_ready"), sem("rstd_ready")
        xh_ready, xn_ready, xn_copied = sem("xh_ready"), sem("xn_ready"), sem("xn_copied")
        a_ready, g_ready, gelu_done, u_ready = sem("a_ready"), sem("g_ready"), sem("gelu_done"), sem("u_ready")
        y2_ready, xt0_done = sem("y2_ready"), sem("xt0_done")
        f_ready, f_copied, f_stats, f_var, f_rstd, f_norm, f_out, s_out = (
            sem(n) for n in ("f_ready", "f_copied", "f_stats", "f_var", "f_rstd", "f_norm", "f_out", "s_out"))

        NCONST = 12

        class Body:

            def __init__(self, eng, l, g, first=False, last=False, g0=False):
                self.l, self.g, self.first, self.last, self.g0 = l, g, first, last, g0
                self.i = l * GROUPS + g
                if not isinstance(self.i, int):
                    self.i = eng.snap(self.i)

            def steps(self, eng):
                for c in range(QUAD):
                    s = self.i * QUAD + c
                    if not isinstance(s, int):
                        s = eng.snap(s)
                    yield c, s

            def has(self, c, back):
                if self.first:
                    return c >= back
                if self.last:
                    return c < back
                return True

            def tile(self, c, back):
                if self.g0:
                    return (c - back) % TILES
                return self.g * QUAD + (c - back)

            ffn = property(lambda self: not self.first)

            def prev_group(self):
                return GROUPS - 1 if self.g0 else self.g - 1

        def wait(eng, s, value):
            if isinstance(value, int) and value <= 0:
                return
            eng.wait_ge(s, value)

        def run(eng, group):
            group(Body(eng, 0, 0, first=True, g0=True))
            with eng.Fori(1, GROUPS) as g:
                group(Body(eng, 0, g))
            with eng.Fori(1, LAYERS) as l:
                group(Body(eng, l, 0, g0=True))
                with eng.Fori(1, GROUPS) as g:
                    group(Body(eng, l, g))
            group(Body(eng, LAYERS, 0, last=True, g0=True))

        block = ctx.enter_context(nc.Block())

        @block.sync
        def _(sp):
            sp.dma_start(xmid[:, :, :], x_d.rearrange("(t p) d -> p t d", p=P)).then_inc(s_const, 16)
            for dst, src in ((ident[:, :], ident_d), (level, level_d), (wvT, wvT_d), (wT, w0T_d),
                             (bv, bv_d.partition_broadcast(P)), (eta_bc[:, :], eta_d.partition_broadcast(P)),
                             (kfac[:, :], kfac_d), (mask_in, mask_d), (rope[:, :, :], rope_d),
                             (qk_scales[:, :, :], scale_d.partition_broadcast(P)),
                             (par[:, :], par_d[0])):
                sp.dma_start(dst, src).then_inc(s_const, 16)
            sp.dma_start(wqk[:, :, :], wqk_d.rearrange("l p n -> p l n")).then_inc(s_wqk, 16)

            def load_m(l):
                sp.dma_start(mvT[:, :, :], mvT_d[bass.ds(l, 1)].rearrange("o p a n -> p (o a) n")).then_inc(mw_ready, 16)
                sp.dma_start(wo[:, :, :], wo_d[bass.ds(l, 1)].rearrange("o (a p) n -> p (o a) n", p=P)).then_inc(mw_ready, 16)

            def load_ffn(l):
                sp.dma_start(w1[:, :], w1_d[bass.ds(l, 1)].rearrange("o p n -> p (o n)")).then_inc(fw_ready, 16)
                sp.dma_start(w2[:, 0:2, :], w2_d[bass.ds(l, 1), 0:256, :].rearrange("o (a p) n -> p (o a) n", p=P)).then_inc(fw_ready, 16)
                sp.dma_start(w2[0:HBLK[2][1], 2, :], w2_d[bass.ds(l, 1), 256:HID, :].rearrange("o p n -> p (o n)")).then_inc(fw_ready, 16)
                sp.dma_start(par[:, :], par_d[bass.ds(l, 1)].rearrange("o p n -> p (o n)")).then_inc(fw_ready, 16)

            wait(sp, s_const, 16 * NCONST)
            load_ffn(0)
            wait(sp, x0_first, GROUPS)

            def group(b):
                if b.last:
                    return
                if b.g0:
                    wait(sp, m_ready, 4 * b.l)
                    load_m(b.l)
                later_layer = not (isinstance(b.l, int) and b.l == 0)
                written = sp.to_reg(b.i - 3) if later_layer else None
                for c, s in b.steps(sp):
                    if b.first:
                        wait(sp, proj_done, s - 1)
                    else:
                        sp.wait_ge(proj_done, s - 1)
                    if later_layer:
                        sp.wait_ge(xt0_done, written)
                    col = PAD - WIN + b.tile(c, 0) * P
                    sp.dma_start(xs[0:64, c % 2, :], x0[0:64, bass.ds(col, WIN + P)]).then_inc(xs_ready[c % 2], 16)
                    sp.dma_start(xs[64:P, c % 2, :], x0[64:P, bass.ds(col - 1, WIN + P)]).then_inc(xs_ready[c % 2], 16)
                if b.g0 and not b.first:
                    sp.wait_ge(xt0_done, b.i)
                    load_ffn(b.l)

            run(sp, group)
            out_v = out_d.rearrange("(t p) d -> p t d", p=P)
            for r in range(GROUPS):
                sp.wait_ge(f_out, r + 1)
                sp.dma_start(out_v[:, QUAD * r:QUAD * r + QUAD, :], xmid[:, QUAD * r:QUAD * r + QUAD, :]).then_inc(s_out, 16)
            sp.wait_ge(s_out, 16 * GROUPS)

        @block.tensor
        def _(pe):
            mm, tr = nc.tensor.matmul, nc.tensor.transpose
            wait(pe, s_const, 16 * NCONST)

            with pe.Fori(0, GROUPS) as gr:
                vbase = pe.snap(gr * DVE1)

                def each(bank, lhsT, rhs, inc=True):
                    for k in range(QUAD):
                        last = mm(bank[:, k, :], lhsT(k), rhs(k), start=True, stop=True)
                    if inc:
                        last.then_inc(pe1, 1)

                pe.wait_ge(ve, vbase + MARK["xn"])
                for k in range(QUAD):
                    last = tr(pbank[0][:, k, :], c_xn[:, k, :], ident[:, :])
                last.then_inc(pe1, 1)
                pe.wait_ge(ve, vbase + MARK["xT"])
                each(pbank[1], lambda k: c_xT[:, k, :], lambda k: c_xT[:, k, :], False)
                each(pbank[2], lambda k: c_xT[:, k, :], lambda k: wvT)
                for n in range(LEVELS - 1):
                    pe.wait_ge(ve, vbase + MARK["m", n])
                    pe.wait_ge(pl1, gr * POOL1 + POOL_B + n + 1)
                    each(pbank[0], lambda k: c_b[n][:, k, :], lambda k: c_mT[:, k, :])
                    pe.wait_ge(ve, vbase + MARK["q", n])
                    each(pbank[1], lambda k: c_q[:, k, :], lambda k: c_m[:, k, :], False)
                    each(pbank[2], lambda k: c_m[:, k, :], lambda k: c_q[:, k, :])
                pe.wait_ge(ve, vbase + MARK["m", LEVELS - 1])
                each(pbank[0], lambda k: c_xn[:, k, :], lambda k: c_mT[:, k, :], False)
                each(pbank[1], lambda k: c_mT[:, k, :], lambda k: c_v[:, k, :])
                for k in range(QUAD):
                    pe.wait_ge(ve, vbase + MARK["w", k])
                    mm(pbank[3][:, k, :], c_pT[:, k, :], wT, start=True, stop=True).then_inc(pe1, 1)
                    pe.wait_ge(ve, vbase + MARK["u", k])
                    mm(pbank[2][:, k, :], c_xn[:, k, :], c_u[:, k, :], start=True, stop=True).then_inc(pe1, 1)
                pe.wait_ge(ve, vbase + MARK["x0n"])
                for k in range(QUAD):
                    last = tr(pbank[0][:, k, :], c_t[:, k, :], ident[:, :])
                last.then_inc(pe1, 1)

            wait(pe, s_wqk, 16)
            wait(pe, s_lmask, 2)
            wait(pe, x0_first, GROUPS)

            def group(b):
                i = b.i
                for c, s in b.steps(pe):
                    def project(n):
                        return mm(psq[:, 512 * n:512 * n + 512], xs[:, c % 2, WIN:WIN + P],
                                  wqk[:, bass.ds(b.l, 1), 512 * n:512 * n + 512].rearrange("p o n -> p (o n)"),
                                  start=True, stop=True)

                    def turn(r):
                        for k in range(4):
                            blk = 4 * ((r + 2) % 4) + k
                            last = tr(pt[r % 2][:, k * P:k * P + P], qn[:, blk * P:blk * P + P], ident[:, :])
                        last.then_inc(qkT_ready, 1)

                    if b.has(c, 0):
                        pe.wait_ge(xs_ready[c % 2], i * 64 + 32 * (c // 2) + 32)
                        if b.has(c, 3):
                            pe.wait_ge(zT_copied, 4 * s - 9)
                        elif c == 1:
                            pe.wait_ge(x_copied, 1)
                        if b.g0 and c == 2:
                            pe.wait_ge(m_copied, 4 * b.l + 3)
                        if b.ffn and c == 2:
                            pe.wait_ge(xf_copied, i)
                        if b.ffn and c == 3:
                            pe.wait_ge(gelu_done, 3 * i)
                        for k in range(2):
                            last = tr(pt[0][:, k * P:k * P + P],
                                      xs[:, c % 2, WIN * k:WIN * k + P], ident[:, :])
                        last.then_inc(x_ready, 1)
                        if not (b.first and c == 0):
                            pe.wait_ge(rope_ab, 2 * s)
                            pe.wait_ge(sq_done, 2 * s)
                        for n in range(3):
                            project(n)
                    if b.has(c, 1):
                        pe.wait_ge(qn_ready, s)
                        if b.has(c, 0):
                            pe.wait_ge(x_copied, s + 1)
                        else:
                            pe.wait_ge(zT_copied, 4 * s - 9)
                        turn(0)
                        if not b.first or c >= 3:
                            pe.wait_ge(y_added, s - 2)
                        if b.ffn and c == 3:
                            pe.wait_ge(u_ready, 3 * i)
                        if b.ffn and c == 0:
                            wait(pe, xt0_done, i - 1)
                        if b.g0 and c == 2:
                            pe.wait_ge(m_copied, 4 * b.l + 4)
                        turn(1)
                    if b.has(c, 0):
                        project(3).then_inc(proj_done, 1)
                    if b.has(c, 1):
                        pe.wait_ge(qkT_copied, 4 * s - 3)
                        turn(2)
                        first_tile = 1 if (b.g0 and c == 1) else 0
                        if not (b.first and c == 1):
                            pe.wait_ge(p_shifted, s - 1)
                        for h in range(2):
                            mm(pss[:, 512 * h:512 * h + 512], ident16[:, :], mask16[:, first_tile, :],
                               start=True, stop=False)
                        pe.wait_ge(qkT_copied, 4 * s - 2)
                        turn(3)
                    if b.has(c, 2):
                        pe.wait_ge(p_ready, s - 1)
                        if b.has(c, 1):
                            pe.wait_ge(kprev_ready, s)
                            pe.wait_ge(qkT_copied, 4 * s)
                        else:
                            pe.wait_ge(zT_copied, 4 * s - 9)
                            pe.wait_ge(y_added, s - 2)
                        for r in range(2):
                            for a in range(4):
                                src = a * 256 + r * 2 * KEYS
                                last = tr(pt[r][:, a * P:a * P + P], pr[:, c % 2, src:src + 2 * KEYS], ident[:, :])
                            last.then_inc(pT_ready, 1)
                    if b.has(c, 1):
                        if not b.has(c, 2):
                            pe.wait_ge(kprev_ready, s)
                            pe.wait_ge(qkT_copied, 4 * s)
                        for n in range(NWIN):
                            w = window_of(n)
                            for a2 in range(2):
                                bank = pss[:, 512 * a2:512 * a2 + 512].rearrange("p (r n j) -> p r n j", r=2, j=KEYS)
                                for g in range(4):
                                    pair = 4 * a2 + g
                                    last = mm(bank[WIN * g:WIN * g + WIN, :, n, :],
                                              qT[:, pair, WIN * w:WIN * w + WIN],
                                              kT[:, (c - 1) % 2, pair, :, WIN * w:WIN * w + KEYS],
                                              start=False, stop=(n == NWIN - 1))
                        last.then_inc(s_ready, 1)
                    if b.has(c, 2):
                        pe.wait_ge(x_copied, s - 1)
                        for n in range(NWIN):
                            if n < 2:
                                pe.wait_ge(pT_copied, 2 * s - 4 + n + 1)
                            else:
                                pe.wait_ge(zT_copied, 4 * s - 8 + n - 1)
                            row = 64 * (n % 2)
                            mm(pt[n % 2][:, :], xw[row:row + KEYS, (c - 2) % 4, n // 2, :],
                               pT[row:row + KEYS, n // 2, :], start=True, stop=True).then_inc(zT_ready, 1)
                        pe.wait_ge(zT_copied, 4 * s - 4)
                        if b.g0 and c == 2:
                            pe.wait_ge(m_copied, 4 * b.l + 4)
                        for n in range(HEADS):
                            last = mm(pt[1][:, 0:P], mh[:, head_of(n // 4, n % 4), :],
                                      zT[:, n, :, :].rearrange("p w i -> p (w i)"),
                                      start=(n == 0), stop=(n == HEADS - 1))
                        last.then_inc(y_ready, 1)
                    if b.g0 and c == 1 and not b.last:
                        pe.wait_ge(mw_ready, 32 * b.l + 32)
                        if not b.first:
                            pe.wait_ge(zT_copied, 4 * s - 5)
                            pe.wait_ge(y_added, s - 1)
                        else:
                            pe.wait_ge(qkT_copied, 4)
                        for r in range(4):
                            if r >= 2:
                                pe.wait_ge(m_copied, 4 * b.l + r - 1)
                            row = 64 * (r % 2)
                            for k in range(4):
                                pair = 4 * (r // 2) + k
                                last = mm(pt[r % 2][:, k * P:k * P + P], mvT[row:row + HD, pair, :],
                                          wo[row:row + HD, pair, :], start=True, stop=True)
                            last.then_inc(m_ready, 1)
                    if b.ffn and c == 1:
                        pe.wait_ge(xs2_ready, i)
                        pe.wait_ge(zT_copied, 4 * s - 5)
                        if b.g0 and not b.last:
                            pe.wait_ge(m_copied, 4 * b.l + 3)
                        for k in range(QUAD):
                            last = tr(pt[0][:, k * P:k * P + P], xs2[:, k * P:k * P + P], ident[:, :])
                        last.then_inc(xf_ready, 1)
                    if b.ffn and c == 2:
                        pe.wait_ge(xh_ready, i)
                        pe.wait_ge(xf_copied, i)
                        if not b.last:
                            pe.wait_ge(zT_copied, 4 * s - 5)
                        for k in range(QUAD):
                            last = tr(pt[0][:, k * P:k * P + P], xh[:, k, :], ident[:, :])
                        last.then_inc(xn_ready, 1)
                        pe.wait_ge(fw_ready, 64 * ((b.l - 1) if b.g0 else b.l) + 64)
                        pe.wait_ge(xn_copied, i)
                        for k, (h0, n) in enumerate(HBLK):
                            if k == 0:
                                pe.wait_ge(y_added, STEPS if b.last else s - 1)
                            else:
                                pe.wait_ge(u_ready, 3 * i - 3 + k)
                            mm(pt[1][0:n, :], w1[:, h0:h0 + n], xnT[:, :], start=True, stop=True).then_inc(a_ready, 1)
                            if k > 0:
                                pe.wait_ge(gelu_done, 3 * i - 3 + k)
                            mm(pt[0][0:n, :], w1[:, HID + h0:HID + h0 + n], xnT[:, :],
                               start=True, stop=True).then_inc(g_ready, 1)
                    if b.ffn and c == 3:
                        pe.wait_ge(u_ready, 3 * i)
                        if not b.last:
                            pe.wait_ge(y_added, s - 1)
                        for k, (h0, n) in enumerate(HBLK):
                            last = mm(pt[1][:, :], w2[0:n, k, :], uT[0:n, k, :], start=(k == 0), stop=(k == 2))
                        last.then_inc(y2_ready, 1)

            run(pe, group)

            for r in range(GROUPS):
                pe.wait_ge(xt0_done, LAYERS * GROUPS)
                if r == 0:
                    pe.wait_ge(gelu_done, 3 * LAYERS * GROUPS)
                if r >= 2:
                    pe.wait_ge(f_copied, r - 1)
                for k in range(QUAD):
                    col = PAD + (QUAD * r + k) * P
                    last = tr(pt[r % 2][:, k * P:k * P + P], x0[:, col:col + P], ident[:, :])
                last.then_inc(f_ready, 1)

        @block.vector
        def _(dve):
            v = nc.vector
            v.memset(neg_half[:, :], -0.5)
            v.memset(eps[:, :], EPS)
            v.memset(x1[:, 0:PAD], 0.0)
            v.memset(x0[:, 0:PAD], 0.0)
            v.memset(coef[:, :], 0.0).then_inc(s_cv, 1)
            wait(dve, s_cv, 1)
            wait(dve, s_const, 16 * NCONST)
            v.tensor_scalar(coef[:, 0:1], eta_bc[:, :], 2.0 / P, None, ALU.mult).then_inc(s_cv, 1)
            dve.wait_ge(s_cv, 2)
            v.tensor_scalar(coef[:, 1:2], coef[:, 0:1], -1.0, None, ALU.mult).then_inc(s_cv, 1)
            dve.wait_ge(s_cv, 3)

            with dve.Fori(0, GROUPS) as gr:
                vbase = dve.snap(gr * DVE1)
                pbase = dve.snap(gr * PE1)
                gbase = dve.snap(gr * POOL1)
                n_ve, n_pe, n_pl = [0], [0], [0]

                def own(ins):
                    n_ve[0] += 1
                    ins.then_inc(ve, 1)
                    dve.wait_ge(ve, vbase + n_ve[0])

                def mark(key):
                    assert MARK[key] == n_ve[0], (key, n_ve[0])

                def after_pe():
                    n_pe[0] += 1
                    dve.wait_ge(pe1, pbase + n_pe[0])

                def after_pool(n):
                    n_pl[0] += n
                    dve.wait_ge(pl1, gbase + n_pl[0])

                def norm(src, dst, whole_src, whole_dst):
                    for k in range(QUAD):
                        ins = v.bn_stats(bst[:, k, :], src(k))
                    own(ins)
                    v.tensor_scalar(whole_dst, whole_src, 1.0, None, ALU.mult)
                    for k in range(QUAD):
                        ins = v.bn_aggr(mv[:, k, :], bst[:, k, :])
                    own(ins)
                    after_pool(2)
                    for k in range(QUAD):
                        ins = v.tensor_scalar(dst(k), dst(k), mv[:, k, 0:1], rstd[:, k:k + 1], ALU.subtract, ALU.mult)
                    own(ins)

                def tiles(t):
                    return t[:, bass.ds(gr * QUAD, QUAD), :]

                def tile_of(t):
                    return lambda k: t[:, bass.ds(gr * QUAD + k, 1), :].rearrange("p o n -> p (o n)")

                norm(tile_of(xmid), lambda k: c_xn[:, k, :], tiles(xmid), c_xn)
                mark("xn")
                after_pe()
                own(v.tensor_copy(c_xT, pbank[0]))
                mark("xT")
                after_pe()
                own(v.tensor_scalar(c_g, pbank[1], coef[:, 0:1], None, ALU.mult))
                own(v.tensor_tensor(c_v, pbank[2], bv.unsqueeze(1).broadcast_to([P, QUAD, P]), ALU.add))
                mark("g")
                idb = ident[:, :].unsqueeze(1).broadcast_to([P, QUAD, P])

                def lev(n):
                    return level[:, n, :].unsqueeze(1).broadcast_to([P, QUAD, P])

                own(v.tensor_tensor(c_m, c_g, lev(0), ALU.mult))
                own(v.tensor_tensor(c_m, idb, c_m, ALU.subtract))
                own(v.tensor_tensor(c_mT, c_g, lev(LEVELS), ALU.mult))
                own(v.tensor_tensor(c_mT, idb, c_mT, ALU.subtract))
                mark(("m", 0))
                n_pl[0] += LEVELS - 1
                for n in range(LEVELS - 1):
                    after_pe()
                    own(v.tensor_copy(c_q, pbank[0]))
                    mark(("q", n))
                    after_pe()
                    own(v.tensor_tensor(c_m, c_m, pbank[1], ALU.subtract))
                    own(v.tensor_tensor(c_mT, c_mT, pbank[2], ALU.subtract))
                    mark(("m", n + 1))
                after_pe()
                own(v.tensor_copy(c_pT, pbank[0]))
                own(v.tensor_copy(c_qp, pbank[1]))
                for k in range(QUAD):
                    mark(("w", k))
                    after_pe()
                    own(v.tensor_tensor(c_u[:, k, :], pbank[3][:, k, :], c_qp[:, k, :], ALU.subtract))
                    mark(("u", k))
                    after_pe()
                    own(v.scalar_tensor_tensor(wT, pbank[2][:, k, :], coef[:, 1:2], wT, ALU.mult, ALU.add))
                own(v.tensor_tensor(c_y, c_u, c_v, ALU.add))
                norm(lambda k: c_y[:, k, :], lambda k: c_t[:, k, :], c_y, c_t)
                own(v.tensor_tensor(c_y, c_t, tiles(xmid), ALU.add))
                v.tensor_scalar(tiles(xmid), c_y, 1.0, None, ALU.mult)
                norm(lambda k: c_y[:, k, :], lambda k: c_t[:, k, :], c_y, c_t)
                mark("x0n")
                after_pe()
                v.tensor_scalar(x0[:, bass.ds(PAD + gr * QUAD * P, QUAD * P)],
                                pbank[0].rearrange("p c n -> p (c n)"), 1.0, None, ALU.mult).then_inc(x0_first, 1)
                assert n_ve[0] == DVE1 and n_pe[0] == PE1 and n_pl[0] == POOL1, (n_ve, n_pe, n_pl)

            dve.wait_ge(x0_first, GROUPS)
            v.memset(kT_flat, 0.0).then_inc(s_kz, 1)
            q3 = psq[:, :].rearrange("p (h d) -> p h d", d=HD)
            a3, b3 = (t[:, :].rearrange("p (h d) -> p h d", d=HD) for t in (qa, qb))
            q4, b4 = (t[:, :].rearrange("p (h a d) -> p h a d", a=2, d=HD // 2) for t in (psq, qb))
            n3 = qn[:, :].rearrange("p (h d) -> p h d", d=HD)

            def group(b):
                i = b.i
                for c, s in b.steps(dve):
                    if b.has(c, 0):
                        if not (b.first and c == 0):
                            dve.wait_ge(rope_ab, 2 * s)
                        v.tensor_tensor(tab[:, :, :].rearrange("p a d -> p (a d)"),
                                        rope[:, bass.ds(b.tile(c, 0), 1), :].rearrange("p o n -> p (o n)"),
                                        qk_scales[:, bass.ds(b.l, 1), :].rearrange("p o n -> p (o n)"),
                                        ALU.mult).then_inc(tab_ready, 1)
                        dve.wait_ge(tab_ready, s + 1)
                        dve.wait_ge(proj_done, s + 1)
                        if not (b.first and c == 0):
                            dve.wait_ge(qn_ready, s)
                            dve.wait_ge(rope_sum, s)
                        for qk in (1, 0):
                            if qk == 0:
                                dve.wait_ge(sq_done, 2 * s + 1)
                            hs = slice(HEADS * qk, HEADS * qk + HEADS)
                            v.tensor_tensor(a3[:, hs, :], q3[:, hs, :],
                                            tab[:, 2 * qk, :].unsqueeze(1).broadcast_to([P, HEADS, HD]), ALU.mult)
                            v.tensor_tensor(
                                b4[:, hs], q4[:, hs, ::-1, :],
                                tab[:, 2 * qk + 1, :].rearrange("p (a d) -> p a d", a=2).unsqueeze(1)
                                .broadcast_to([P, HEADS, 2, 32]), ALU.mult).then_inc(rope_ab, 1)
                        dve.wait_ge(sq_done, 2 * s + 2)
                        if not (b.first and c == 0):
                            dve.wait_ge(r_ready, s)
                        v.tensor_reduce(ss[:, :], sq[:, :].rearrange("p (h d) -> p h d", d=HD),
                                        AX.X, ALU.add).then_inc(ss_ready, 1)
                        dve.wait_ge(ss_ready, s + 1)
                        v.tensor_scalar(ssc[:, :], ss[:, :], 1e-24, None, ALU.max).then_inc(ssc_ready, 1)
                    if b.has(c, 1):
                        p4 = pr[:, (c - 1) % 2, :].rearrange("p (h j) -> p h j", j=KEYS)
                        dve.wait_ge(s_ready, s)
                        if not (b.first and c == 1):
                            dve.wait_ge(p_shifted, s - 1)
                        v.tensor_reduce(mx[:, :], pss[:, :].rearrange("p (h j) -> p h j", j=KEYS),
                                        AX.X, ALU.max).then_inc(mx_ready, 1)
                        dve.wait_ge(mx_ready, s)
                        if not (b.first and c <= 2):
                            dve.wait_ge(pT_ready, 2 * s - 4)
                        v.tensor_tensor(p4, pss[:, :].rearrange("p (h j) -> p h j", j=KEYS),
                                        mx[:, :].unsqueeze(2).broadcast_to([P, HEADS, KEYS]),
                                        ALU.subtract).then_inc(p_shifted, 1)
                        dve.wait_ge(exp_done, s)
                        v.tensor_reduce(den[:, :], p4, AX.X, ALU.add).then_inc(den_ready, 1)
                        dve.wait_ge(den_ready, s)
                        if not (b.first and c == 1):
                            dve.wait_ge(p_ready, s - 1)
                        v.reciprocal(rden[:, :], den[:, :]).then_inc(rden_ready, 1)
                    if b.ffn and c == 2:
                        wait(dve, xn_ready, i - 1)
                        dve.wait_ge(xf_copied, i)
                        dve.wait_ge(rstd_ready, i)
                        for k in range(QUAD):
                            last = v.tensor_scalar(xh[:, k, :], xf[:, k, :], mv[:, k, 0:1], rstd[:, k:k + 1],
                                                   ALU.subtract, ALU.mult)
                        last.then_inc(xh_ready, 1)
                    if b.has(c, 2):
                        dve.wait_ge(y_ready, s - 1)
                        col = PAD + b.tile(c, 2) * P
                        v.tensor_tensor(x1[:, bass.ds(col, P)], pt[1][:, 0:P], x0[:, bass.ds(col, P)],
                                        ALU.add).then_inc(y_added, 1)
                    if b.has(c, 0):
                        dve.wait_ge(rope_sum, s + 1)
                        dve.wait_ge(r_ready, s + 1)
                        if not (b.first and c == 0):
                            dve.wait_ge(qkT_ready, 4 * s)
                        v.tensor_tensor(n3, a3, rn[:, :].unsqueeze(2).broadcast_to([P, 2 * HEADS, HD]),
                                        ALU.mult).then_inc(qn_ready, 1)
                    if b.ffn and c == 1:
                        dve.wait_ge(y_added, s - 1)
                        wait(dve, g_ready, 3 * i - 3)
                        col = PAD + b.prev_group() * 512
                        v.tensor_copy(xs2[0:64, :], x1[0:64, bass.ds(col, 512)])
                        v.tensor_copy(xs2[64:P, :], x1[64:P, bass.ds(col - 1, 512)]).then_inc(xs2_ready, 1)
                        dve.wait_ge(xf_ready, i)
                        for k in range(QUAD):
                            last = v.bn_stats(bst[:, k, :], pt[0][:, k * P:k * P + P])
                        last.then_inc(bst_ready, 1)
                        wait(dve, xn_ready, i - 1)
                        wait(dve, rstd_ready, i - 1)
                        dve.wait_ge(bst_ready, i)
                        v.tensor_copy(xf[:, :, :].rearrange("p c n -> p (c n)"), pt[0][:, :]).then_inc(xf_copied, 1)
                        for k in range(QUAD):
                            last = v.bn_aggr(mv[:, k, :], bst[:, k, :])
                        last.then_inc(mv_ready, 1)
                    if b.ffn and c == 2:
                        dve.wait_ge(xn_ready, i)
                        dve.wait_ge(fw_ready, 64 * ((b.l - 1) if b.g0 else b.l) + 64)
                        v.tensor_scalar(xnT[:, :], pt[0][:, :], par[:, 0:1], par[:, 1:2],
                                        ALU.mult, ALU.add).then_inc(xn_copied, 1)
                        wait(dve, y2_ready, i - 1)
                        for k, (h0, n) in enumerate(HBLK):
                            dve.wait_ge(a_ready, 3 * i - 3 + k + 1)
                            dve.wait_ge(gelu_done, 3 * i - 3 + k + 1)
                            v.scalar_tensor_tensor(uT[0:n, k, :], pt[1][0:n, :], par[0:n, 2 + k:3 + k],
                                                   gl[0:n, k % 2, :], ALU.add, ALU.mult).then_inc(u_ready, 1)
                    if b.ffn and c == 3:
                        dve.wait_ge(y2_ready, i)
                        dve.wait_ge(xs_ready[0], 16 * STEPS if b.last else i * 64 + 32)
                        col = PAD + b.prev_group() * 512
                        v.scalar_tensor_tensor(x0[:, bass.ds(col, 512)], pt[1][:, :], par[:, 8:9],
                                               x1[:, bass.ds(col, 512)], ALU.add, ALU.add).then_inc(xt0_done, 1)

            run(dve, group)

            for r in range(GROUPS):
                dve.wait_ge(f_ready, r + 1)
                wait(dve, f_out, r)
                v.tensor_copy(xf[:, :, :].rearrange("p c n -> p (c n)"), pt[r % 2][:, :]).then_inc(f_copied, 1)
                dve.wait_ge(f_copied, r + 1)
                for k in range(QUAD):
                    last = v.bn_stats(bst[:, k, :], xf[:, k, :])
                last.then_inc(f_stats, 1)
                dve.wait_ge(f_stats, 2 * r + 1)
                for k in range(QUAD):
                    last = v.bn_aggr(mv[:, k, :], bst[:, k, :])
                last.then_inc(f_stats, 1)
                dve.wait_ge(f_rstd, r + 1)
                for k in range(QUAD):
                    last = v.tensor_scalar(xh[:, k, :], xf[:, k, :], mv[:, k, 0:1], rstd[:, k:k + 1],
                                           ALU.subtract, ALU.mult)
                last.then_inc(f_norm, 1)
                dve.wait_ge(f_norm, r + 1)
                part = xmid[:, QUAD * r:QUAD * r + QUAD, :]
                v.tensor_tensor(part, xh[:, :, :], part, ALU.add).then_inc(f_out, 1)

        @block.scalar
        def _(act):
            wait(act, s_const, 16 * NCONST)
            nc.scalar.copy(mask16[:, :, :], mask_in).then_inc(s_lmask, 1)
            nc.scalar.copy(ident16[:, :], ident[:, :]).then_inc(s_lmask, 1)
            wait(act, s_lmask, 2)
            wait(act, x0_first, GROUPS)
            wait(act, s_cv, 1)
            wait(act, s_kz, 1)

            def group(b):
                i = b.i
                for c, s in b.steps(act):
                    if b.has(c, 0):
                        act.wait_ge(x_ready, s + 1)
                        if not b.first:
                            act.wait_ge(zT_ready, 4 * s - 12)
                        nc.scalar.copy(xw[:, c, :, :].rearrange("p a n -> p (a n)"), pt[0][:, 0:2 * P]).then_inc(x_copied, 1)
                    if b.has(c, 1):
                        slot, other = (c - 1) % 2, c % 2
                        if not (b.first and c == 1):
                            act.wait_ge(s_ready, s - 1)
                            act.wait_ge(qkT_copied, 4 * s - 4)
                        for r in range(2):
                            rows = slice(HD * r, HD * r + HD)
                            last = nc.scalar.activation(kT[rows, slot, :, r, 0:WIN], kT[rows, other, :, r, P:P + WIN],
                                                        ACT.Copy, scale=kfac[rows, 0:1])
                        last.then_inc(kprev_ready, 1)
                        for t in range(4):
                            act.wait_ge(qkT_ready, 4 * s - 4 + t + 1)
                            src = pt[t % 2][:, :].rearrange("p (k n) -> p k n", k=4)
                            pairs = slice(4 * (t % 2), 4 * (t % 2) + 4)
                            if t >= 2:
                                last = nc.scalar.copy(qT[:, pairs, :], src)
                            else:
                                for r in range(2):
                                    rows = slice(HD * r, HD * r + HD)
                                    last = nc.scalar.copy(kT[rows, slot, pairs, r, WIN:WIN + P], src[rows])
                            last.then_inc(qkT_copied, 1)
                    if b.has(c, 0):
                        act.wait_ge(proj_done, s + 1)
                        if not (b.first and c == 0):
                            act.wait_ge(ss_ready, s)
                            act.wait_ge(qkT_ready, 4 * s)
                        nc.scalar.activation(sq[:, 0:1024], psq[:, 0:1024], ACT.Square).then_inc(sq_done, 1)
                    if b.has(c, 2):
                        if not (b.first and c == 2):
                            act.wait_ge(zT_ready, 4 * s - 8)
                        for r in range(2):
                            act.wait_ge(pT_ready, 2 * s - 4 + r + 1)
                            nc.scalar.copy(pT[:, r, :], pt[r][:, :]).then_inc(pT_copied, 1)
                    if b.has(c, 0):
                        act.wait_ge(rope_ab, 2 * s + 1)
                        nc.scalar.activation(sq[:, 1024:2048], psq[:, 1024:2048], ACT.Square).then_inc(sq_done, 1)
                    if b.has(c, 2):
                        if not (b.first and c == 2):
                            act.wait_ge(y_ready, s - 2)
                        for n in range(NWIN):
                            act.wait_ge(zT_ready, 4 * s - 8 + n + 1)
                            nc.scalar.copy(zT[:, :, window_of(n), :],
                                           pt[n % 2][:, :].rearrange("p (h i) -> p h i", i=WIN)).then_inc(zT_copied, 1)
                    if b.has(c, 1):
                        act.wait_ge(p_shifted, s)
                        part = pr[:, (c - 1) % 2, :]
                        nc.scalar.activation(part, part, ACT.Exp, scale=QK_SCALE).then_inc(exp_done, 1)
                    if b.g0 and c == 1 and not b.last:
                        if not b.first:
                            act.wait_ge(y_ready, s - 1)
                        for r in range(4):
                            act.wait_ge(m_ready, 4 * b.l + r + 1)
                            h0 = 8 * (r // 2) + r % 2
                            nc.scalar.copy(mh[:, h0:h0 + 7:2, :], pt[r % 2][:, :].rearrange("p (k n) -> p k n", k=4)).then_inc(m_copied, 1)
                    if b.ffn and c == 2:
                        act.wait_ge(fw_ready, 64 * ((b.l - 1) if b.g0 else b.l) + 64)
                        for k, (h0, n) in enumerate(HBLK):
                            act.wait_ge(g_ready, 3 * i - 3 + k + 1)
                            wait(act, u_ready, 3 * i - 3 + max(k - 1, 0))
                            nc.scalar.activation(gl[0:n, k % 2, :], pt[0][0:n, :], ACT.Gelu,
                                                 bias=par[0:n, 5 + k:6 + k]).then_inc(gelu_done, 1)

            run(act, group)

        @block.gpsimd
        def _(pool):
            g_ = nc.gpsimd
            wait(pool, s_cv, 1)
            wait(pool, s_const, 16 * NCONST)
            with pool.Fori(0, GROUPS) as gr:
                vbase = pool.snap(gr * DVE1)
                gbase = pool.snap(gr * POOL1)
                n_pl = [0]

                def root(mark):
                    pool.wait_ge(ve, vbase + mark)
                    g_.tensor_tensor(vare[:, :], mv[:, :, 1:2].rearrange("p k o -> p (k o)"), eps[:, :], ALU.add).then_inc(pl1, 1)
                    n_pl[0] += 1
                    pool.wait_ge(pl1, gbase + n_pl[0])
                    g_.tensor_tensor(rstd[:, :], vare[:, :], neg_half[:, 0:QUAD], ALU.pow).then_inc(pl1, 1)
                    n_pl[0] += 1

                root(MARK["xn"] - 1)
                pool.wait_ge(ve, vbase + MARK["g"])
                for n in range(LEVELS - 1):
                    g_.tensor_tensor(c_b[n], c_g, level[:, n + 1, :].unsqueeze(1).broadcast_to([P, QUAD, P]),
                                     ALU.mult).then_inc(pl1, 1)
                    n_pl[0] += 1
                root(MARK["yn"])
                root(MARK["x0n"] - 1)
                assert n_pl[0] == POOL1

            wait(pool, x0_first, GROUPS)

            def group(b):
                i = b.i
                for c, s in b.steps(pool):
                    if b.has(c, 0):
                        for half in (1, 0):
                            pool.wait_ge(rope_ab, 2 * s + 2 - half)
                            part = slice(1024 * half, 1024 * half + 1024)
                            last = g_.tensor_tensor(qa[:, part], qa[:, part], qb[:, part], ALU.add)
                        last.then_inc(rope_sum, 1)
                        if not (b.first and c == 0):
                            pool.wait_ge(qn_ready, s)
                        pool.wait_ge(ssc_ready, s + 1)
                        g_.tensor_tensor(rn[:, :], ssc[:, :], neg_half[:, :], ALU.pow).then_inc(r_ready, 1)
                    if b.has(c, 1):
                        pool.wait_ge(rden_ready, s)
                        p4 = pr[:, (c - 1) % 2, :].rearrange("p (h j) -> p h j", j=KEYS)
                        g_.tensor_tensor(p4, p4, rden[:, :].unsqueeze(2).broadcast_to([P, HEADS, KEYS]),
                                         ALU.mult).then_inc(p_ready, 1)
                    if b.ffn and c == 1:
                        pool.wait_ge(mv_ready, i)
                        g_.tensor_tensor(vare[:, :], mv[:, :, 1:2].rearrange("p k o -> p (k o)"), eps[:, :], ALU.add).then_inc(vare_ready, 1)
                        pool.wait_ge(vare_ready, i)
                        wait(pool, xh_ready, i - 1)
                        g_.tensor_tensor(rstd[:, :], vare[:, :], neg_half[:, 0:QUAD], ALU.pow).then_inc(rstd_ready, 1)

            run(pool, group)
            for r in range(GROUPS):
                pool.wait_ge(f_stats, 2 * r + 2)
                g_.tensor_tensor(vare[:, :], mv[:, :, 1:2].rearrange("p k o -> p (k o)"), eps[:, :], ALU.add).then_inc(f_var, 1)
                pool.wait_ge(f_var, r + 1)
                g_.tensor_tensor(rstd[:, :], vare[:, :], neg_half[:, 0:QUAD], ALU.pow).then_inc(f_rstd, 1)


def window_of(n):
    return 2 * (n % 2) + n // 2


MARK = {"xn": 3, "xT": 4, "g": 6, ("m", 0): 10}
for _n in range(LEVELS - 1):
    MARK["q", _n] = MARK["m", _n] + 1
    MARK["m", _n + 1] = MARK["m", _n] + 3
MARK["w", 0] = MARK["m", LEVELS - 1] + 2
for _k in range(QUAD):
    MARK["u", _k] = MARK["w", _k] + 1
    MARK["w", _k + 1] = MARK["w", _k] + 2
MARK["yn"] = MARK["w", QUAD] + 3
MARK["x0n"] = MARK["yn"] + 5
DVE1 = MARK["x0n"]
PE1 = 2 + 2 * (LEVELS - 1) + 1 + 2 * QUAD + 1
POOL_B = 2
POOL1 = 6 + LEVELS - 1


def constants():
    import numpy as np
    ident = np.eye(P, dtype=np.float32)
    i = (np.arange(P) % WIN)[:, None]
    j = np.arange(KEYS)[None, :]
    hide = (i < j - WIN) | (i > j)
    mask = np.zeros((P, 2, 2, NWIN, KEYS), np.float32)
    mask[:, :, :, :, :] = np.where(hide, np.float32(-1e30), np.float32(0))[:, None, None, None, :]
    mask[:, 1, :, 0, :WIN] = -1e30
    half = np.arange(0, HD, 2, dtype=np.float64)
    inv_freq = (1.0 / np.float32(10000.0) ** (half.astype(np.float32) / np.float32(HD))).astype(np.float32)
    t = np.arange(TOKENS, dtype=np.float32)
    freqs = (t[:, None] * inv_freq[None, :]).astype(np.float64)
    base = (half + 0.4 * HD) / (1.4 * HD)
    power = ((np.arange(TOKENS) % P) - P // 2)[:, None] / (WIN // 2)
    scale = base[None, :] ** power
    cos, sin = np.cos(freqs), np.sin(freqs)
    tabs = []
    for sc in (scale, 1.0 / scale):
        tabs.append(np.concatenate([cos * sc, cos * sc], -1))
        tabs.append(np.concatenate([-sin * sc, sin * sc], -1))
    rope = np.stack(tabs, 1).astype(np.float32)
    rope = np.ascontiguousarray(rope.reshape(TILES, P, 4 * HD).transpose(1, 0, 2))
    kfac = np.tile(np.concatenate([base, base]) ** (P // (WIN // 2)), 2).astype(np.float32)[:, None]
    r, c = np.arange(P)[:, None], np.arange(P)[None, :]
    lev = []
    for n in range(LEVELS):
        b = 2 ** n
        lev.append(((r // (2 * b)) == (c // (2 * b))) & ((r // b) % 2 == 1) & ((c // b) % 2 == 0))
    lev.append(lev[0].T)
    level = np.ascontiguousarray(np.stack(lev, 1).astype(np.float32))
    return ident, np.ascontiguousarray(mask.reshape(P, 2, 512)), rope, kfac, level


def kernel(L0_attn_x, L0_attn_W0, L0_attn_Wkv, L0_attn_bkv, L0_attn_eta, L0_ffn_Wqkv, L0_ffn_q_scale,
           L0_ffn_k_scale, L0_ffn_Wo, L0_ffn_ln_g, L0_ffn_ln_b, L0_ffn_W1, L0_ffn_b1, L0_ffn_W2, L0_ffn_b2):
    import numpy as np
    import concourse.bacc as bacc
    from concourse.bass_utils import run_bass_kernel_spmd

    ident, mask, rope, kfac, level = constants()
    f = lambda a: np.ascontiguousarray(np.asarray(a))
    wqkv, qs, ks = f(L0_ffn_Wqkv), f(L0_ffn_q_scale), f(L0_ffn_k_scale)
    swap = lambda a: np.concatenate([a[:, HD // 2:], a[:, :HD // 2]], 1)
    inner = HEADS * HD
    par = np.zeros((LAYERS, P, 9), np.float32)
    par[:, :, 0], par[:, :, 1], par[:, :, 8] = f(L0_ffn_ln_g), f(L0_ffn_ln_b), f(L0_ffn_b2)
    b1 = f(L0_ffn_b1)
    for k, (h0, n) in enumerate(HBLK):
        par[:, :n, 2 + k] = b1[:, h0:h0 + n]
        par[:, :n, 5 + k] = b1[:, HID + h0:HID + h0 + n]
    arrays = {
        "x": f(L0_attn_x)[0],
        "wvT": f(f(L0_attn_Wkv)[P:, :].T),
        "w0T": f(f(L0_attn_W0).T),
        "bv": f(L0_attn_bkv)[P:],
        "eta": f(L0_attn_eta).reshape(1),
        "wqk": f(wqkv[:, :, :2 * inner]),
        "scales": f(np.stack([qs, swap(qs), ks, swap(ks)], 1).reshape(LAYERS, 4 * HD)),
        "mvT": f(wqkv[:, :, 2 * inner:].transpose(0, 2, 1).reshape(LAYERS, PAIRS, P, P).transpose(0, 2, 1, 3)),
        "wo": f(L0_ffn_Wo),
        "w1": f(L0_ffn_W1),
        "w2": f(L0_ffn_W2),
        "par": par,
        "ident": ident, "mask": mask, "rope": rope, "kfac": kfac, "level": level,
    }
    nc = bacc.Bacc("TRN2", target_bir_lowering=False, num_devices=1)
    ins = [nc.dram_tensor(f"in_{n}", a.shape, F32, kind="ExternalInput").ap() for n, a in arrays.items()]
    out = nc.dram_tensor("out", (TOKENS, P), F32, kind="ExternalOutput").ap()
    build(nc, *ins, out)
    res = run_bass_kernel_spmd(nc, [{f"in_{n}": a for n, a in arrays.items()}], core_ids=[0])
    return res.results[0]["out"].reshape(1, TOKENS, P)
```

```python
from contextlib import ExitStack

import concourse.bass as bass
from concourse import mybir

F32 = mybir.dt.float32
BF16 = mybir.dt.bfloat16
ALU = mybir.AluOpType
ACT = mybir.ActivationFunctionType
AX = mybir.AxisListType

P = 128
TOKENS = 2048
TILES = TOKENS // P
LAYERS = 6
QUAD = 4
GROUPS = TILES // QUAD
STEPS = LAYERS * TILES
HEADS, HD, WIN = 16, 64, 32
NWIN = P // WIN
KEYS = 2 * WIN
PAIRS = HEADS // 2
HID = 341
HBLK = [(0, 128), (128, 128), (256, HID - 256)]
PAD = 64
EPS = 1e-5
QK_SCALE = 8.0
LEVELS = 7


def head_of(a, g):
    return 2 * (4 * (a // 2) + g) + a % 2


def build(nc, x_d, wvT_d, w0T_d, bv_d, eta_d, wqk_d, scale_d, mvT_d, wo_d, w1_d, w2_d, par_d,
          ident_d, mask_d, rope_d, kfac_d, level_d, out_d):
    ctx = ExitStack()
    with ctx:
        def sb(name, shape, dt=F32):
            return ctx.enter_context(nc.sbuf_tensor(name, shape, dt))

        def sem(name):
            return ctx.enter_context(nc.semaphore(name))

        ident = sb("ident", [P, P])
        ident16 = sb("ident16", [P, P], BF16)
        mask16 = sb("mask16", [P, 2, 512], BF16)
        rope = sb("rope", [P, TILES, 4 * HD])
        kfac = sb("kfac", [P, 1])
        qk_scales = sb("qk_scales", [P, LAYERS, 4 * HD])
        wqk = sb("wqk", [P, LAYERS, 2 * HEADS * HD])
        neg_half = sb("neg_half", [P, 2 * HEADS])
        eps = sb("eps", [P, QUAD])
        eta_bc = sb("eta_bc", [P, 1])
        coef = sb("coef", [P, 2])
        x0 = sb("x0", [P, PAD + TOKENS])
        x1 = sb("x1", [P, PAD + TOKENS])
        xmid = sb("xmid", [P, TILES, P])
        mvT = sb("mvT", [P, PAIRS, P])
        wo = sb("wo", [P, PAIRS, P])
        mh = sb("mh", [P, HEADS, P])
        w1 = sb("w1", [P, 2 * HID])
        w2 = sb("w2", [P, 3, P])
        par = sb("par", [P, 9])
        xs = sb("xs", [P, 2, WIN + P])
        xw = sb("xw", [P, 4, 2, P])
        tab = sb("tab", [P, 4, HD])
        qa = sb("qa", [P, 2048])
        qb = sb("qb", [P, 2048])
        qn = sb("qn", [P, 2048])
        sq = qn
        ss = sb("ss", [P, 2 * HEADS])
        ssc = sb("ssc", [P, 2 * HEADS])
        rn = sb("rn", [P, 2 * HEADS])
        qT = sb("qT", [P, PAIRS, P])
        kT = sb("kT", [P, 2, PAIRS, 2, WIN + P])
        mx = sb("mx", [P, HEADS])
        den = sb("den", [P, HEADS])
        rden = sb("rden", [P, HEADS])
        pr = sb("pr", [P, 2, 1024])
        pT = sb("pT", [P, 2, 512])
        zT = sb("zT", [P, HEADS, NWIN, WIN])
        xs2 = sb("xs2", [P, 512])
        xf = sb("xf", [P, QUAD, P])
        xh = xf
        xnT = xs2
        bst = sb("bst", [P, QUAD, 6])
        mv = sb("mv", [P, QUAD, 2])
        vare = sb("vare", [P, QUAD])
        rstd = sb("rstd", [P, QUAD])
        gl = sb("gl", [P, 2, 512])
        uT = sb("uT", [P, 3, 512])
        kT_flat = kT[:, :, :, :, :].rearrange("p s a r n -> p (s a r n)")
        c_xn, c_xT, c_g, c_v = (kT_flat[:, 512 * i:512 * i + 512].rearrange("p (c n) -> p c n", c=4) for i in range(4))
        c_mm = qn[:, 0:1024].rearrange("p (f t k n) -> p f t k n", f=2, t=2, k=2)
        c_q, c_u = (qn[:, 512 * i:512 * i + 512].rearrange("p (c n) -> p c n", c=4) for i in (2, 3))
        c_b = [(qa, qb)[i // 4][:, 512 * (i % 4):512 * (i % 4) + 512].rearrange("p (c n) -> p c n", c=4)
               for i in range(LEVELS - 1)]
        c_pT, c_qp = (pr[:, 0, 512 * i:512 * i + 512].rearrange("p (c n) -> p c n", c=4) for i in range(2))
        c_y, c_t = (pr[:, 1, 512 * i:512 * i + 512].rearrange("p (c n) -> p c n", c=4) for i in range(2))
        wT = uT[:, 0, 0:P]
        wvT = uT[:, 0, P:2 * P]
        bv = uT[:, 0, 2 * P:3 * P]
        level = mh[:, 0:LEVELS + 1, :]
        mask_in = zT[:, 0:8, :, :].rearrange("p h w i -> p (h w i)").rearrange("p (v n) -> p v n", v=2)

        psq = ctx.enter_context(nc.psum_tensor("psq", [P, 2048], F32))
        pt = [ctx.enter_context(nc.psum_tensor(f"pt{i}", [P, 512], F32)) for i in range(2)]
        pss = ctx.enter_context(nc.psum_tensor("pss", [P, 1024], F32))
        pbank = [psq[:, 512 * i:512 * i + 512].rearrange("p (c n) -> p c n", c=4) for i in range(4)]

        m_bank = [pt[0], pss[:, 0:512], pss[:, 512:1024], pt[1]]

        s_const = sem("s_const")
        s_tables = sem("s_tables")
        s_wqk = sem("s_wqk")
        s_cv = sem("s_cv")
        s_lmask = sem("s_lmask")
        ve = sem("ve")
        pe1 = sem("pe1")
        pl1 = sem("pl1")
        s_kz = sem("s_kz")
        x0_first = sem("x0_first")
        xs_ready = [sem(f"xs_ready{k}") for k in range(2)]
        x_ready, x_copied = sem("x_ready"), sem("x_copied")
        projk_done, proj_done = sem("projk_done"), sem("proj_done")
        sq_done, ss_ready, ssc_ready, r_ready = sem("sq_done"), sem("ss_ready"), sem("ssc_ready"), sem("r_ready")
        tab_ready, rope_ab, rope_sum, qn_ready = sem("tab_ready"), sem("rope_ab"), sem("rope_sum"), sem("qn_ready")
        qkT_ready, qkT_copied, kprev_ready = sem("qkT_ready"), sem("qkT_copied"), sem("kprev_ready")
        s_ready, mx_ready, p_shifted, exp_done = sem("s_ready"), sem("mx_ready"), sem("p_shifted"), sem("exp_done")
        den_ready, rden_ready, p_ready = sem("den_ready"), sem("rden_ready"), sem("p_ready")
        pT_ready, pT_copied = sem("pT_ready"), sem("pT_copied")
        zT_ready, zT_copied = sem("zT_ready"), sem("zT_copied")
        y_ready, y_added = sem("y_ready"), sem("y_added")
        mw_ready, m_ready, m_copied = sem("mw_ready"), sem("m_ready"), sem("m_copied")
        fw_ready = sem("fw_ready")
        xs2_ready, xf_ready, xf_copied = sem("xs2_ready"), sem("xf_ready"), sem("xf_copied")
        bst_ready, mv_ready, vare_ready, rstd_ready = sem("bst_ready"), sem("mv_ready"), sem("vare_ready"), sem("rstd_ready")
        xh_ready, xn_ready, xn_copied = sem("xh_ready"), sem("xn_ready"), sem("xn_copied")
        a_ready, g_ready, gelu_done, u_ready = sem("a_ready"), sem("g_ready"), sem("gelu_done"), sem("u_ready")
        y2_ready, xt0_done = sem("y2_ready"), sem("xt0_done")
        f_ready, f_copied, f_stats, f_var, f_rstd, f_norm, f_out, s_out = (
            sem(n) for n in ("f_ready", "f_copied", "f_stats", "f_var", "f_rstd", "f_norm", "f_out", "s_out"))

        NCONST, NTABLES = 7, 4

        class Body:

            def __init__(self, eng, l, g, first=False, last=False, g0=False):
                self.l, self.g, self.first, self.last, self.g0 = l, g, first, last, g0
                self.i = l * GROUPS + g
                if not isinstance(self.i, int):
                    self.i = eng.snap(self.i)

            def steps(self, eng):
                for c in range(QUAD):
                    s = self.i * QUAD + c
                    if not isinstance(s, int):
                        s = eng.snap(s)
                    yield c, s

            def has(self, c, back):
                if self.first:
                    return c >= back
                if self.last:
                    return c < back
                return True

            def tile(self, c, back):
                if self.g0:
                    return (c - back) % TILES
                return self.g * QUAD + (c - back)

            ffn = property(lambda self: not self.first)

            def prev_group(self):
                return GROUPS - 1 if self.g0 else self.g - 1

        def wait(eng, s, value):
            if isinstance(value, int) and value <= 0:
                return
            eng.wait_ge(s, value)

        def min_steps(b, value):
            return min(value, STEPS) if b.last else value

        def run(eng, group):
            group(Body(eng, 0, 0, first=True, g0=True))
            with eng.Fori(1, GROUPS) as g:
                group(Body(eng, 0, g))
            with eng.Fori(1, LAYERS) as l:
                group(Body(eng, l, 0, g0=True))
                with eng.Fori(1, GROUPS) as g:
                    group(Body(eng, l, g))
            group(Body(eng, LAYERS, 0, last=True, g0=True))

        def load_ffn(eng, l):
            eng.dma_start(w1[:, :], w1_d[bass.ds(l, 1)].rearrange("o p n -> p (o n)")).then_inc(fw_ready, 16)
            eng.dma_start(w2[:, 0:2, :], w2_d[bass.ds(l, 1), 0:256, :].rearrange("o (a p) n -> p (o a) n", p=P)).then_inc(fw_ready, 16)
            eng.dma_start(w2[0:HBLK[2][1], 2, :], w2_d[bass.ds(l, 1), 256:HID, :].rearrange("o p n -> p (o n)")).then_inc(fw_ready, 16)
            eng.dma_start(par[:, :], par_d[bass.ds(l, 1)].rearrange("o p n -> p (o n)")).then_inc(fw_ready, 16)

        block = ctx.enter_context(nc.Block())

        @block.sync
        def _(sp):
            for dst, src in ((xmid[:, :, :], x_d.rearrange("(t p) d -> p t d", p=P)),
                             (ident[:, :], ident_d), (wvT, wvT_d), (eta_bc[:, :], eta_d.partition_broadcast(P)),
                             (level, level_d), (wT, w0T_d), (bv, bv_d.partition_broadcast(P))):
                sp.dma_start(dst, src).then_inc(s_const, 16)
            for dst, src in ((kfac[:, :], kfac_d), (mask_in, mask_d), (rope[:, :, :], rope_d),
                             (qk_scales[:, :, :], scale_d.partition_broadcast(P))):
                sp.dma_start(dst, src).then_inc(s_tables, 16)
            sp.dma_start(wqk[:, :, :], wqk_d.rearrange("l p n -> p l n")).then_inc(s_wqk, 16)

            def load_m(l):
                sp.dma_start(mvT[:, :, :], mvT_d[bass.ds(l, 1)].rearrange("o p a n -> p (o a) n")).then_inc(mw_ready, 16)
                sp.dma_start(wo[:, :, :], wo_d[bass.ds(l, 1)].rearrange("o (a p) n -> p (o a) n", p=P)).then_inc(mw_ready, 16)

            load_ffn(sp, 0)
            wait(sp, x0_first, GROUPS)

            def group(b):
                if b.last:
                    return
                if b.g0:
                    wait(sp, m_ready, 4 * b.l)
                    load_m(b.l)
                later_layer = not (isinstance(b.l, int) and b.l == 0)
                written = sp.to_reg(b.i - 3) if later_layer else None
                for c, s in b.steps(sp):
                    if b.first:
                        wait(sp, proj_done, s - 1)
                    else:
                        sp.wait_ge(proj_done, s - 1)
                    if later_layer:
                        sp.wait_ge(xt0_done, written)
                    col = PAD - WIN + b.tile(c, 0) * P
                    sp.dma_start(xs[0:64, c % 2, :], x0[0:64, bass.ds(col, WIN + P)]).then_inc(xs_ready[c % 2], 16)
                    sp.dma_start(xs[64:P, c % 2, :], x0[64:P, bass.ds(col - 1, WIN + P)]).then_inc(xs_ready[c % 2], 16)

            run(sp, group)
            out_v = out_d.rearrange("(t p) d -> p t d", p=P)
            for r in range(GROUPS):
                sp.wait_ge(f_out, r + 1)
                sp.dma_start(out_v[:, QUAD * r:QUAD * r + QUAD, :], xmid[:, QUAD * r:QUAD * r + QUAD, :]).then_inc(s_out, 16)
            sp.wait_ge(s_out, 16 * GROUPS)

        @block.tensor
        def _(pe):
            mm, tr = nc.tensor.matmul, nc.tensor.transpose
            wait(pe, s_const, 16 * NCONST)

            with pe.Fori(0, GROUPS) as gr:
                vbase = pe.snap(gr * DVE1)

                def each(bank, lhsT, rhs, inc=True):
                    for k in range(QUAD):
                        last = mm(bank[:, k, :], lhsT(k), rhs(k), start=True, stop=True)
                    if inc:
                        last.then_inc(pe1, 1)

                pe.wait_ge(ve, vbase + MARK["xn"])
                for k in range(QUAD):
                    last = tr(pbank[0][:, k, :], c_xn[:, k, :], ident[:, :])
                last.then_inc(pe1, 1)
                pe.wait_ge(ve, vbase + MARK["xT"])
                each(pbank[1], lambda k: c_xT[:, k, :], lambda k: c_xT[:, k, :], False)
                each(pbank[2], lambda k: c_xT[:, k, :], lambda k: wvT)
                for n in range(LEVELS - 1):
                    for f in range(2):
                        pe.wait_ge(ve, vbase + MARK["m", n, f])
                        if f == 0:
                            pe.wait_ge(pl1, gr * POOL1 + POOL_B + n + 1)
                        for k in range(2):
                            last = mm(pbank[2 * f][:, k, :], c_b[n][:, 2 * f + k, :], c_mm[:, f, 1, k, :],
                                      start=True, stop=True)
                        last.then_inc(pe1, 1)
                    for f in range(2):
                        pe.wait_ge(ve, vbase + MARK["q", n, f])
                        for k in range(2):
                            mm(pbank[2 * f + 1][:, k, :], c_q[:, 2 * f + k, :], c_mm[:, f, 0, k, :],
                               start=True, stop=True)
                            last = mm(pbank[2 * f + 1][:, 2 + k, :], c_mm[:, f, 0, k, :], c_q[:, 2 * f + k, :],
                                      start=True, stop=True)
                        last.then_inc(pe1, 1)
                pe.wait_ge(ve, vbase + MARK["m", LEVELS - 1, 1])
                each(pbank[0], lambda k: c_xn[:, k, :], lambda k: c_mm[:, k // 2, 1, k % 2, :], False)
                each(pbank[1], lambda k: c_mm[:, k // 2, 1, k % 2, :], lambda k: c_v[:, k, :])
                for k in range(QUAD):
                    pe.wait_ge(ve, vbase + MARK["w", k])
                    mm(pbank[3][:, k, :], c_pT[:, k, :], wT, start=True, stop=True).then_inc(pe1, 1)
                    pe.wait_ge(ve, vbase + MARK["u", k])
                    mm(pbank[2][:, k, :], c_xn[:, k, :], c_u[:, k, :], start=True, stop=True).then_inc(pe1, 1)
                pe.wait_ge(ve, vbase + MARK["x0n"])
                for k in range(QUAD):
                    last = tr(pbank[0][:, k, :], c_t[:, k, :], ident[:, :])
                last.then_inc(pe1, 1)

            wait(pe, s_wqk, 16)
            wait(pe, s_lmask, 2)
            wait(pe, x0_first, GROUPS)

            def group(b):
                i = b.i
                for c, s in b.steps(pe):
                    def project(n):
                        return mm(psq[:, 512 * n:512 * n + 512], xs[:, c % 2, WIN:WIN + P],
                                  wqk[:, bass.ds(b.l, 1), 512 * n:512 * n + 512].rearrange("p o n -> p (o n)"),
                                  start=True, stop=True)

                    def merge(r):
                        row = 64 * (r % 2)
                        for k in range(4):
                            pair = 4 * (r // 2) + k
                            last = mm(m_bank[r][:, k * P:k * P + P], mvT[row:row + HD, pair, :],
                                      wo[row:row + HD, pair, :], start=True, stop=True)
                        last.then_inc(m_ready, 1)

                    last_later = b.has(c, 1) and b.has(c, 2) and not (b.ffn and c == 3)

                    def score(n):
                        w = window_of(n)
                        for a2 in range(2):
                            bank = pss[:, 512 * a2:512 * a2 + 512].rearrange("p (r n j) -> p r n j", r=2, j=KEYS)
                            for g in range(4):
                                pair = 4 * a2 + g
                                last = mm(bank[WIN * g:WIN * g + WIN, :, n, :],
                                          qT[:, pair, WIN * w:WIN * w + WIN],
                                          kT[:, (c - 1) % 2, pair, :, WIN * w:WIN * w + KEYS],
                                          start=False, stop=(n == NWIN - 1))
                        if n == NWIN - 1:
                            last.then_inc(s_ready, 1)

                    def hidden(bank, k, gate):
                        h0, n = HBLK[k]
                        col = h0 + gate * HID
                        mm(bank[0:n, :], w1[:, col:col + n], xnT[:, :], start=True,
                           stop=True).then_inc(g_ready if gate else a_ready, 1)

                    def turn(r):
                        for k in range(4):
                            blk = 4 * ((r + 2) % 4) + k
                            last = tr(pt[r % 2][:, k * P:k * P + P], qn[:, blk * P:blk * P + P], ident[:, :])
                        last.then_inc(qkT_ready, 1)

                    if b.has(c, 0):
                        pe.wait_ge(xs_ready[c % 2], i * 64 + 32 * (c // 2) + 32)
                        if b.has(c, 3):
                            pe.wait_ge(zT_copied, 4 * s - 9)
                        elif c == 1:
                            pe.wait_ge(x_copied, 1)
                        if b.g0 and c == 2:
                            pe.wait_ge(m_copied, 4 * b.l + 1)
                        if b.ffn and c == 3:
                            pe.wait_ge(xn_copied, i)
                        if b.ffn and c == 0:
                            wait(pe, gelu_done, 3 * i - 3)
                        for k in range(2):
                            last = tr(pt[0][:, k * P:k * P + P],
                                      xs[:, c % 2, WIN * k:WIN * k + P], ident[:, :])
                        last.then_inc(x_ready, 1)
                        if not (b.first and c == 0):
                            pe.wait_ge(rope_ab, 2 * s)
                            pe.wait_ge(sq_done, 2 * s)
                        project(2)
                    if b.ffn and c == 3:
                        pe.wait_ge(y_added, STEPS if b.last else s - 2)
                        hidden(pt[1], 1, 1)
                    if b.has(c, 0):
                        project(3).then_inc(projk_done, 1)
                        project(0)
                    if b.ffn and c == 2:
                        pe.wait_ge(xs2_ready, i)
                        pe.wait_ge(p_shifted, min_steps(b, s - 1))
                        if b.g0 and not b.last:
                            pe.wait_ge(m_copied, 4 * b.l + 2)
                        for k in range(QUAD):
                            last = tr(pss[:, k * P:k * P + P], xs2[:, k * P:k * P + P], ident[:, :])
                        last.then_inc(xf_ready, 1)
                    if b.ffn and c == 3:
                        pe.wait_ge(u_ready, 3 * i - 2)
                        hidden(pss[:, 0:512], 1, 0)
                    if b.has(c, 1):
                        pe.wait_ge(qn_ready, s)
                        if b.has(c, 0):
                            pe.wait_ge(x_copied, s + 1)
                        else:
                            pe.wait_ge(zT_copied, 4 * s - 9)
                        turn(0)
                        if not b.first or c >= 3:
                            pe.wait_ge(y_added, s - 2)
                        if b.ffn and c == 3:
                            pe.wait_ge(gelu_done, 3 * i - 1)
                        if b.g0 and c == 2:
                            pe.wait_ge(m_copied, 4 * b.l + 4)
                        turn(1)
                    if b.has(c, 0):
                        project(1).then_inc(proj_done, 1)
                    if b.has(c, 1):
                        pe.wait_ge(qkT_copied, 4 * s - 3)
                        turn(2)
                        first_tile = 1 if (b.g0 and c == 1) else 0
                        if not (b.first and c == 1):
                            pe.wait_ge(p_shifted, s - 1)
                        if b.g0 and c == 2 and not b.last:
                            pe.wait_ge(m_copied, 4 * b.l + 4)
                        if b.ffn and c == 2:
                            pe.wait_ge(xf_copied, i)
                        if b.ffn and c == 3:
                            pe.wait_ge(u_ready, 3 * i - 1)
                        if b.ffn and c == 0:
                            wait(pe, xt0_done, i - 1)
                        for h in range(2):
                            mm(pss[:, 512 * h:512 * h + 512], ident16[:, :], mask16[:, first_tile, :],
                               start=True, stop=False)
                        pe.wait_ge(qkT_copied, 4 * s - 2)
                        turn(3)
                    if b.has(c, 2):
                        pe.wait_ge(p_ready, s - 1)
                        for r in range(2):
                            if b.has(c, 1):
                                pe.wait_ge(qkT_copied, 4 * s - 1 + r)
                                if r == 1:
                                    pe.wait_ge(kprev_ready, s)
                            elif r == 0:
                                pe.wait_ge(zT_copied, 4 * s - 9)
                            else:
                                pe.wait_ge(y_added, s - 2)
                            for a in range(4):
                                src = a * 256 + r * 2 * KEYS
                                last = tr(pt[r][:, a * P:a * P + P], pr[:, c % 2, src:src + 2 * KEYS], ident[:, :])
                            last.then_inc(pT_ready, 1)
                    if b.has(c, 1):
                        if not b.has(c, 2):
                            pe.wait_ge(kprev_ready, s)
                            pe.wait_ge(qkT_copied, 4 * s)
                        for n in range(NWIN - 1 if last_later else NWIN):
                            score(n)
                    if b.has(c, 2):
                        pe.wait_ge(x_copied, s - 1)
                        for n in range(NWIN):
                            if n < 2:
                                pe.wait_ge(pT_copied, 2 * s - 4 + n + 1)
                            else:
                                pe.wait_ge(zT_copied, 4 * s - 8 + n - 1)
                            row = 64 * (n % 2)
                            mm(pt[n % 2][:, :], xw[row:row + KEYS, (c - 2) % 4, n // 2, :],
                               pT[row:row + KEYS, n // 2, :], start=True, stop=True).then_inc(zT_ready, 1)
                    if b.ffn and c == 2:
                        pe.wait_ge(xh_ready, i)
                        pe.wait_ge(zT_copied, 4 * STEPS if b.last else 4 * s - 5)
                        for k in range(QUAD):
                            last = tr(pt[0][:, k * P:k * P + P], xh[:, k, :], ident[:, :])
                        last.then_inc(xn_ready, 1)
                    if b.ffn and c == 3:
                        pe.wait_ge(zT_copied, 4 * STEPS if b.last else 4 * s - 5)
                        hidden(pt[0], 2, 1)
                        pe.wait_ge(p_shifted, min_steps(b, s))
                        if b.last:
                            pe.wait_ge(u_ready, 3 * i - 1)
                        hidden(pss[:, 0:512], 2, 0)
                    if last_later:
                        score(NWIN - 1)
                    if b.g0 and c == 1 and not b.last:
                        pe.wait_ge(mw_ready, 32 * b.l + 32)
                        if b.first:
                            pe.wait_ge(qkT_copied, 4)
                        else:
                            pe.wait_ge(zT_copied, 4 * s - 5)
                        merge(0)
                    if b.has(c, 2):
                        pe.wait_ge(zT_copied, 4 * s - 4)
                        if b.g0 and c == 2:
                            pe.wait_ge(m_copied, 4 * b.l + 4)
                        for n in range(HEADS):
                            last = mm(pt[1][:, 0:P], mh[:, head_of(n // 4, n % 4), :],
                                      zT[:, n, :, :].rearrange("p w i -> p (w i)"),
                                      start=(n == 0), stop=(n == HEADS - 1))
                        last.then_inc(y_ready, 1)
                    if b.g0 and c == 1 and not b.last:
                        pe.wait_ge(p_shifted, s)
                        merge(1)
                        merge(2)
                        if not b.first:
                            pe.wait_ge(y_added, s - 1)
                        merge(3)
                    if b.ffn and c == 2:
                        pe.wait_ge(xn_copied, i)
                        pe.wait_ge(fw_ready, 64 * ((b.l - 1) if b.g0 else b.l) + 64)
                        pe.wait_ge(p_shifted, min_steps(b, s))
                        hidden(pss[:, 0:512], 0, 0)
                        hidden(pss[:, 512:1024], 0, 1)
                    if b.ffn and c == 3:
                        pe.wait_ge(u_ready, 3 * i)
                        pe.wait_ge(p_shifted, min_steps(b, s))
                        for k, (h0, n) in enumerate(HBLK):
                            last = mm(pss[:, 512:1024], w2[0:n, k, :], uT[0:n, k, :], start=(k == 0), stop=(k == 2))
                        last.then_inc(y2_ready, 1)

            run(pe, group)

            for r in range(GROUPS):
                pe.wait_ge(xt0_done, LAYERS * GROUPS)
                if r == 0:
                    pe.wait_ge(gelu_done, 3 * LAYERS * GROUPS)
                if r >= 2:
                    pe.wait_ge(f_copied, r - 1)
                for k in range(QUAD):
                    col = PAD + (QUAD * r + k) * P
                    last = tr(pt[r % 2][:, k * P:k * P + P], x0[:, col:col + P], ident[:, :])
                last.then_inc(f_ready, 1)

        @block.vector
        def _(dve):
            v = nc.vector
            v.memset(neg_half[:, :], -0.5)
            v.memset(eps[:, :], EPS)
            v.memset(x1[:, 0:PAD], 0.0)
            v.memset(x0[:, 0:PAD], 0.0)
            v.memset(coef[:, :], 0.0).then_inc(s_cv, 1)
            wait(dve, s_cv, 1)
            wait(dve, s_const, 16 * NCONST)
            v.tensor_scalar(coef[:, 0:1], eta_bc[:, :], 2.0 / P, None, ALU.mult).then_inc(s_cv, 1)
            dve.wait_ge(s_cv, 2)
            v.tensor_scalar(coef[:, 1:2], coef[:, 0:1], -1.0, None, ALU.mult).then_inc(s_cv, 1)
            dve.wait_ge(s_cv, 3)

            with dve.Fori(0, GROUPS) as gr:
                vbase = dve.snap(gr * DVE1)
                pbase = dve.snap(gr * PE1)
                gbase = dve.snap(gr * POOL1)
                n_ve, n_pe, n_pl = [0], [0], [0]

                def own(ins):
                    n_ve[0] += 1
                    ins.then_inc(ve, 1)
                    dve.wait_ge(ve, vbase + n_ve[0])

                def mark(key):
                    assert MARK[key] == n_ve[0], (key, n_ve[0])

                def after_pe():
                    n_pe[0] += 1
                    dve.wait_ge(pe1, pbase + n_pe[0])

                def after_pool(n):
                    n_pl[0] += n
                    dve.wait_ge(pl1, gbase + n_pl[0])

                def norm(src, dst, whole_src, whole_dst):
                    for k in range(QUAD):
                        ins = v.bn_stats(bst[:, k, :], src(k))
                    own(ins)
                    v.tensor_scalar(whole_dst, whole_src, 1.0, None, ALU.mult)
                    for k in range(QUAD):
                        ins = v.bn_aggr(mv[:, k, :], bst[:, k, :])
                    own(ins)
                    after_pool(2)
                    for k in range(QUAD):
                        ins = v.tensor_scalar(dst(k), dst(k), mv[:, k, 0:1], rstd[:, k:k + 1], ALU.subtract, ALU.mult)
                    own(ins)

                def tiles(t):
                    return t[:, bass.ds(gr * QUAD, QUAD), :]

                def tile_of(t):
                    return lambda k: t[:, bass.ds(gr * QUAD + k, 1), :].rearrange("p o n -> p (o n)")

                norm(tile_of(xmid), lambda k: c_xn[:, k, :], tiles(xmid), c_xn)
                mark("xn")
                after_pe()
                own(v.tensor_copy(c_xT, pbank[0]))
                mark("xT")
                after_pe()
                own(v.tensor_scalar(c_g, pbank[1], coef[:, 0:1], None, ALU.mult))
                own(v.tensor_tensor(c_v, pbank[2], bv.unsqueeze(1).broadcast_to([P, QUAD, P]), ALU.add))
                mark("g")
                def halves(t):
                    if len(t.shape) == 2:
                        return t.unsqueeze(1).unsqueeze(1).broadcast_to([P, 2, 2, P])
                    return t.rearrange("p (f k) n -> p f k n", f=2)

                for t, lev in ((0, 0), (1, LEVELS)):
                    own(v.tensor_tensor(c_mm[:, :, t], halves(c_g), halves(level[:, lev, :]), ALU.mult))
                    own(v.tensor_tensor(c_mm[:, :, t], halves(ident[:, :]), c_mm[:, :, t], ALU.subtract))
                mark(("m", 0, 1))
                n_pl[0] += LEVELS - 1
                for n in range(LEVELS - 1):
                    for f in range(2):
                        after_pe()
                        own(v.tensor_copy(c_q[:, 2 * f:2 * f + 2, :], pbank[2 * f][:, 0:2, :]))
                        mark(("q", n, f))
                    for f in range(2):
                        after_pe()
                        both = c_mm[:, f].rearrange("p t k n -> p (t k n)")
                        own(v.tensor_tensor(both, both, pbank[2 * f + 1].rearrange("p c n -> p (c n)"), ALU.subtract))
                        mark(("m", n + 1, f))
                after_pe()
                own(v.tensor_copy(c_pT, pbank[0]))
                own(v.tensor_copy(c_qp, pbank[1]))
                for k in range(QUAD):
                    mark(("w", k))
                    after_pe()
                    own(v.tensor_tensor(c_u[:, k, :], pbank[3][:, k, :], c_qp[:, k, :], ALU.subtract))
                    mark(("u", k))
                    after_pe()
                    own(v.scalar_tensor_tensor(wT, pbank[2][:, k, :], coef[:, 1:2], wT, ALU.mult, ALU.add))
                own(v.tensor_tensor(c_y, c_u, c_v, ALU.add))
                norm(lambda k: c_y[:, k, :], lambda k: c_t[:, k, :], c_y, c_t)
                own(v.tensor_tensor(c_y, c_t, tiles(xmid), ALU.add))
                v.tensor_scalar(tiles(xmid), c_y, 1.0, None, ALU.mult)
                norm(lambda k: c_y[:, k, :], lambda k: c_t[:, k, :], c_y, c_t)
                mark("x0n")
                after_pe()
                v.tensor_scalar(x0[:, bass.ds(PAD + gr * QUAD * P, QUAD * P)],
                                pbank[0].rearrange("p c n -> p (c n)"), 1.0, None, ALU.mult).then_inc(x0_first, 1)
                assert n_ve[0] == DVE1 and n_pe[0] == PE1 and n_pl[0] == POOL1, (n_ve, n_pe, n_pl)

            dve.wait_ge(x0_first, GROUPS)
            wait(dve, s_tables, 16 * NTABLES)
            v.memset(kT_flat, 0.0).then_inc(s_kz, 1)
            q3 = psq[:, :].rearrange("p (h d) -> p h d", d=HD)
            a3, b3 = (t[:, :].rearrange("p (h d) -> p h d", d=HD) for t in (qa, qb))
            q4, b4 = (t[:, :].rearrange("p (h a d) -> p h a d", a=2, d=HD // 2) for t in (psq, qb))
            n3 = qn[:, :].rearrange("p (h d) -> p h d", d=HD)

            def group(b):
                i = b.i
                for c, s in b.steps(dve):
                    def gated(k, bank):
                        n = HBLK[k][1]
                        dve.wait_ge(a_ready, 3 * i - 3 + k + 1)
                        dve.wait_ge(gelu_done, 3 * i - 3 + k + 1)
                        v.scalar_tensor_tensor(uT[0:n, k, :], bank[0:n, :], par[0:n, 2 + k:3 + k],
                                               gl[0:n, k % 2, :], ALU.add, ALU.mult).then_inc(u_ready, 1)

                    if b.has(c, 0):
                        if not (b.first and c == 0):
                            dve.wait_ge(rope_ab, 2 * s)
                        v.tensor_tensor(tab[:, :, :].rearrange("p a d -> p (a d)"),
                                        rope[:, bass.ds(b.tile(c, 0), 1), :].rearrange("p o n -> p (o n)"),
                                        qk_scales[:, bass.ds(b.l, 1), :].rearrange("p o n -> p (o n)"),
                                        ALU.mult).then_inc(tab_ready, 1)
                        dve.wait_ge(tab_ready, s + 1)
                    if b.ffn and c == 2:
                        dve.wait_ge(xf_ready, i)
                        for k in range(QUAD):
                            last = v.bn_stats(bst[:, k, :], pss[:, k * P:k * P + P])
                        last.then_inc(bst_ready, 1)
                        wait(dve, xn_ready, i - 1)
                        wait(dve, rstd_ready, i - 1)
                        dve.wait_ge(bst_ready, i)
                        v.tensor_copy(xf[:, :, :].rearrange("p c n -> p (c n)"), pss[:, 0:512]).then_inc(xf_copied, 1)
                        for k in range(QUAD):
                            last = v.bn_aggr(mv[:, k, :], bst[:, k, :])
                        last.then_inc(mv_ready, 1)
                    if b.ffn and c == 3:
                        wait(dve, y2_ready, i - 1)
                        gated(0, pss[:, 0:512])
                        gated(1, pss[:, 0:512])
                    if b.has(c, 0):
                        if not (b.first and c == 0):
                            dve.wait_ge(qn_ready, s)
                            dve.wait_ge(rope_sum, s)
                        for qk in (1, 0):
                            dve.wait_ge(projk_done if qk else proj_done, s + 1)
                            hs = slice(HEADS * qk, HEADS * qk + HEADS)
                            v.tensor_tensor(a3[:, hs, :], q3[:, hs, :],
                                            tab[:, 2 * qk, :].unsqueeze(1).broadcast_to([P, HEADS, HD]), ALU.mult)
                            v.tensor_tensor(
                                b4[:, hs], q4[:, hs, ::-1, :],
                                tab[:, 2 * qk + 1, :].rearrange("p (a d) -> p a d", a=2).unsqueeze(1)
                                .broadcast_to([P, HEADS, 2, 32]), ALU.mult).then_inc(rope_ab, 1)
                        if not (b.first and c == 0):
                            dve.wait_ge(r_ready, s)
                        for qk in (1, 0):
                            dve.wait_ge(sq_done, 2 * s + 2 - qk)
                            v.tensor_reduce(ss[:, HEADS * qk:HEADS * qk + HEADS],
                                            sq[:, 1024 * qk:1024 * qk + 1024].rearrange("p (h d) -> p h d", d=HD),
                                            AX.X, ALU.add).then_inc(ss_ready, 1)
                        dve.wait_ge(ss_ready, 2 * s + 2)
                        v.tensor_scalar(ssc[:, :], ss[:, :], 1e-24, None, ALU.max).then_inc(ssc_ready, 1)
                    if b.ffn and c == 2:
                        dve.wait_ge(xf_copied, i)
                        dve.wait_ge(rstd_ready, i)
                        for k in range(QUAD):
                            last = v.tensor_scalar(xh[:, k, :], xf[:, k, :], mv[:, k, 0:1], rstd[:, k:k + 1],
                                                   ALU.subtract, ALU.mult)
                        last.then_inc(xh_ready, 1)
                    if b.has(c, 1):
                        p4 = pr[:, (c - 1) % 2, :].rearrange("p (h j) -> p h j", j=KEYS)
                        dve.wait_ge(s_ready, s)
                        if not (b.first and c == 1):
                            dve.wait_ge(p_shifted, s - 1)
                        v.tensor_reduce(mx[:, :], pss[:, :].rearrange("p (h j) -> p h j", j=KEYS),
                                        AX.X, ALU.max).then_inc(mx_ready, 1)
                        dve.wait_ge(mx_ready, s)
                        if not (b.first and c <= 2):
                            dve.wait_ge(pT_ready, 2 * s - 4)
                        v.tensor_tensor(p4, pss[:, :].rearrange("p (h j) -> p h j", j=KEYS),
                                        mx[:, :].unsqueeze(2).broadcast_to([P, HEADS, KEYS]),
                                        ALU.subtract).then_inc(p_shifted, 1)
                    if b.ffn and c == 2:
                        dve.wait_ge(xn_ready, i)
                        dve.wait_ge(fw_ready, 64 * ((b.l - 1) if b.g0 else b.l) + 64)
                        v.tensor_scalar(xnT[:, :], pt[0][:, :], par[:, 0:1], par[:, 1:2],
                                        ALU.mult, ALU.add).then_inc(xn_copied, 1)
                    if b.ffn and c == 3:
                        gated(2, pss[:, 0:512])
                    if b.has(c, 0):
                        dve.wait_ge(rope_sum, s + 1)
                        dve.wait_ge(r_ready, s + 1)
                        if not (b.first and c == 0):
                            dve.wait_ge(qkT_ready, 4 * s)
                        v.tensor_tensor(n3, a3, rn[:, :].unsqueeze(2).broadcast_to([P, 2 * HEADS, HD]),
                                        ALU.mult).then_inc(qn_ready, 1)
                    if b.has(c, 2):
                        dve.wait_ge(y_ready, s - 1)
                        col = PAD + b.tile(c, 2) * P
                        v.tensor_tensor(x1[:, bass.ds(col, P)], pt[1][:, 0:P], x0[:, bass.ds(col, P)],
                                        ALU.add).then_inc(y_added, 1)
                    if b.has(c, 1):
                        dve.wait_ge(exp_done, s)
                        v.tensor_reduce(den[:, :], p4, AX.X, ALU.add).then_inc(den_ready, 1)
                        dve.wait_ge(den_ready, s)
                        if not (b.first and c == 1):
                            dve.wait_ge(p_ready, s - 1)
                        v.reciprocal(rden[:, :], den[:, :]).then_inc(rden_ready, 1)
                    if b.ffn and c == 3:
                        dve.wait_ge(y2_ready, i)
                        dve.wait_ge(xs_ready[0], 16 * STEPS if b.last else i * 64 + 32)
                        col = PAD + b.prev_group() * 512
                        v.scalar_tensor_tensor(x0[:, bass.ds(col, 512)], pss[:, 512:1024], par[:, 8:9],
                                               x1[:, bass.ds(col, 512)], ALU.add, ALU.add).then_inc(xt0_done, 1)

            run(dve, group)

            for r in range(GROUPS):
                dve.wait_ge(f_ready, r + 1)
                wait(dve, f_out, r)
                v.tensor_copy(xf[:, :, :].rearrange("p c n -> p (c n)"), pt[r % 2][:, :]).then_inc(f_copied, 1)
                dve.wait_ge(f_copied, r + 1)
                for k in range(QUAD):
                    last = v.bn_stats(bst[:, k, :], xf[:, k, :])
                last.then_inc(f_stats, 1)
                dve.wait_ge(f_stats, 2 * r + 1)
                for k in range(QUAD):
                    last = v.bn_aggr(mv[:, k, :], bst[:, k, :])
                last.then_inc(f_stats, 1)
                dve.wait_ge(f_rstd, r + 1)
                for k in range(QUAD):
                    last = v.tensor_scalar(xh[:, k, :], xf[:, k, :], mv[:, k, 0:1], rstd[:, k:k + 1],
                                           ALU.subtract, ALU.mult)
                last.then_inc(f_norm, 1)
                dve.wait_ge(f_norm, r + 1)
                part = xmid[:, QUAD * r:QUAD * r + QUAD, :]
                v.tensor_tensor(part, xh[:, :, :], part, ALU.add).then_inc(f_out, 1)

        @block.scalar
        def _(act):
            wait(act, s_const, 16 * NCONST)
            wait(act, s_tables, 16 * NTABLES)
            nc.scalar.copy(mask16[:, :, :], mask_in).then_inc(s_lmask, 1)
            nc.scalar.copy(ident16[:, :], ident[:, :]).then_inc(s_lmask, 1)
            wait(act, s_lmask, 2)
            wait(act, x0_first, GROUPS)
            wait(act, s_cv, 1)
            wait(act, s_kz, 1)

            def group(b):
                i = b.i
                for c, s in b.steps(act):
                    def gelu(k, bank):
                        n = HBLK[k][1]
                        act.wait_ge(g_ready, 3 * i - 3 + k + 1)
                        wait(act, u_ready, 3 * i - 3 + max(k - 1, 0))
                        nc.scalar.activation(gl[0:n, k % 2, :], bank[0:n, :], ACT.Gelu,
                                             bias=par[0:n, 5 + k:6 + k]).then_inc(gelu_done, 1)

                    if b.has(c, 0):
                        act.wait_ge(x_ready, s + 1)
                        if not b.first:
                            act.wait_ge(zT_ready, 4 * s - 12)
                        nc.scalar.copy(xw[:, c, :, :].rearrange("p a n -> p (a n)"), pt[0][:, 0:2 * P]).then_inc(x_copied, 1)
                    if b.ffn and c == 3:
                        gelu(1, pt[1])
                    if b.has(c, 1):
                        slot, other = (c - 1) % 2, c % 2
                        if not (b.first and c == 1):
                            act.wait_ge(s_ready, s - 1)
                            act.wait_ge(qkT_copied, 4 * s - 4)
                        for r in range(2):
                            rows = slice(HD * r, HD * r + HD)
                            last = nc.scalar.activation(kT[rows, slot, :, r, 0:WIN], kT[rows, other, :, r, P:P + WIN],
                                                        ACT.Copy, scale=kfac[rows, 0:1])
                        last.then_inc(kprev_ready, 1)
                        for t in range(4):
                            act.wait_ge(qkT_ready, 4 * s - 4 + t + 1)
                            src = pt[t % 2][:, :].rearrange("p (k n) -> p k n", k=4)
                            pairs = slice(4 * (t % 2), 4 * (t % 2) + 4)
                            if t >= 2:
                                last = nc.scalar.copy(qT[:, pairs, :], src)
                            else:
                                for r in range(2):
                                    rows = slice(HD * r, HD * r + HD)
                                    last = nc.scalar.copy(kT[rows, slot, pairs, r, WIN:WIN + P], src[rows])
                            last.then_inc(qkT_copied, 1)
                    if b.has(c, 0):
                        if not (b.first and c == 0):
                            act.wait_ge(ss_ready, 2 * s)
                            act.wait_ge(qkT_ready, 4 * s)
                        act.wait_ge(rope_ab, 2 * s + 1)
                        nc.scalar.activation(sq[:, 1024:2048], psq[:, 1024:2048], ACT.Square).then_inc(sq_done, 1)
                    if b.has(c, 2):
                        if not (b.first and c == 2):
                            act.wait_ge(zT_ready, 4 * s - 8)
                        for r in range(2):
                            act.wait_ge(pT_ready, 2 * s - 4 + r + 1)
                            nc.scalar.copy(pT[:, r, :], pt[r][:, :]).then_inc(pT_copied, 1)
                    if b.has(c, 0):
                        act.wait_ge(rope_ab, 2 * s + 2)
                        nc.scalar.activation(sq[:, 0:1024], psq[:, 0:1024], ACT.Square).then_inc(sq_done, 1)
                    if b.has(c, 2):
                        if not (b.first and c == 2):
                            act.wait_ge(y_ready, s - 2)
                        for n in range(NWIN):
                            act.wait_ge(zT_ready, 4 * s - 8 + n + 1)
                            nc.scalar.copy(zT[:, :, window_of(n), :],
                                           pt[n % 2][:, :].rearrange("p (h i) -> p h i", i=WIN)).then_inc(zT_copied, 1)
                    if b.ffn and c == 3:
                        gelu(2, pt[0])
                    if b.has(c, 1):
                        act.wait_ge(p_shifted, s)
                        part = pr[:, (c - 1) % 2, :]
                        nc.scalar.activation(part, part, ACT.Exp, scale=QK_SCALE).then_inc(exp_done, 1)
                    if b.g0 and c == 1 and not b.last:
                        if not b.first:
                            act.wait_ge(y_ready, s - 1)
                        for r in range(4):
                            act.wait_ge(m_ready, 4 * b.l + r + 1)
                            h0 = 8 * (r // 2) + r % 2
                            nc.scalar.copy(mh[:, h0:h0 + 7:2, :], m_bank[r][:, :].rearrange("p (k n) -> p k n", k=4)).then_inc(m_copied, 1)
                    if b.ffn and c == 1:
                        act.wait_ge(y_added, s - 1)
                        wait(act, a_ready, 3 * i - 3)
                        wait(act, g_ready, 3 * i - 3)
                        col = PAD + b.prev_group() * 512
                        nc.scalar.copy(xs2[0:64, :], x1[0:64, bass.ds(col, 512)])
                        nc.scalar.copy(xs2[64:P, :], x1[64:P, bass.ds(col - 1, 512)]).then_inc(xs2_ready, 1)
                    if b.ffn and c == 2:
                        act.wait_ge(fw_ready, 64 * ((b.l - 1) if b.g0 else b.l) + 64)
                        gelu(0, pss[:, 512:1024])
                if b.g0 and not b.first and not b.last:
                    act.wait_ge(xt0_done, i)
                    load_ffn(act, b.l)

            run(act, group)

        @block.gpsimd
        def _(pool):
            g_ = nc.gpsimd
            wait(pool, s_cv, 1)
            wait(pool, s_const, 16 * NCONST)
            with pool.Fori(0, GROUPS) as gr:
                vbase = pool.snap(gr * DVE1)
                gbase = pool.snap(gr * POOL1)
                n_pl = [0]

                def root(mark):
                    pool.wait_ge(ve, vbase + mark)
                    g_.tensor_tensor(vare[:, :], mv[:, :, 1:2].rearrange("p k o -> p (k o)"), eps[:, :], ALU.add).then_inc(pl1, 1)
                    n_pl[0] += 1
                    pool.wait_ge(pl1, gbase + n_pl[0])
                    g_.tensor_tensor(rstd[:, :], vare[:, :], neg_half[:, 0:QUAD], ALU.pow).then_inc(pl1, 1)
                    n_pl[0] += 1

                root(MARK["xn"] - 1)
                pool.wait_ge(ve, vbase + MARK["g"])
                for n in range(LEVELS - 1):
                    g_.tensor_tensor(c_b[n], c_g, level[:, n + 1, :].unsqueeze(1).broadcast_to([P, QUAD, P]),
                                     ALU.mult).then_inc(pl1, 1)
                    n_pl[0] += 1
                root(MARK["yn"])
                root(MARK["x0n"] - 1)
                assert n_pl[0] == POOL1

            wait(pool, x0_first, GROUPS)

            def group(b):
                i = b.i
                for c, s in b.steps(pool):
                    if b.ffn and c == 2:
                        pool.wait_ge(mv_ready, i)
                        g_.tensor_tensor(vare[:, :], mv[:, :, 1:2].rearrange("p k o -> p (k o)"), eps[:, :], ALU.add).then_inc(vare_ready, 1)
                        pool.wait_ge(vare_ready, i)
                        wait(pool, xh_ready, i - 1)
                        g_.tensor_tensor(rstd[:, :], vare[:, :], neg_half[:, 0:QUAD], ALU.pow).then_inc(rstd_ready, 1)
                    if b.has(c, 0):
                        for half in (1, 0):
                            pool.wait_ge(rope_ab, 2 * s + 2 - half)
                            part = slice(1024 * half, 1024 * half + 1024)
                            last = g_.tensor_tensor(qa[:, part], qa[:, part], qb[:, part], ALU.add)
                        last.then_inc(rope_sum, 1)
                        if not (b.first and c == 0):
                            pool.wait_ge(qn_ready, s)
                        pool.wait_ge(ssc_ready, s + 1)
                        g_.tensor_tensor(rn[:, :], ssc[:, :], neg_half[:, :], ALU.pow).then_inc(r_ready, 1)
                    if b.has(c, 1):
                        pool.wait_ge(rden_ready, s)
                        p4 = pr[:, (c - 1) % 2, :].rearrange("p (h j) -> p h j", j=KEYS)
                        g_.tensor_tensor(p4, p4, rden[:, :].unsqueeze(2).broadcast_to([P, HEADS, KEYS]),
                                         ALU.mult).then_inc(p_ready, 1)
            run(pool, group)
            for r in range(GROUPS):
                pool.wait_ge(f_stats, 2 * r + 2)
                g_.tensor_tensor(vare[:, :], mv[:, :, 1:2].rearrange("p k o -> p (k o)"), eps[:, :], ALU.add).then_inc(f_var, 1)
                pool.wait_ge(f_var, r + 1)
                g_.tensor_tensor(rstd[:, :], vare[:, :], neg_half[:, 0:QUAD], ALU.pow).then_inc(f_rstd, 1)


def window_of(n):
    return 2 * (n % 2) + n // 2


MARK = {"xn": 3, "xT": 4, "g": 6, ("m", 0, 0): 10, ("m", 0, 1): 10}
for _n in range(LEVELS - 1):
    for _f in range(2):
        MARK["q", _n, _f] = MARK["m", _n, 1] + 1 + _f
        MARK["m", _n + 1, _f] = MARK["m", _n, 1] + 3 + _f
MARK["w", 0] = MARK["m", LEVELS - 1, 1] + 2
for _k in range(QUAD):
    MARK["u", _k] = MARK["w", _k] + 1
    MARK["w", _k + 1] = MARK["w", _k] + 2
MARK["yn"] = MARK["w", QUAD] + 3
MARK["x0n"] = MARK["yn"] + 5
DVE1 = MARK["x0n"]
PE1 = 2 + 4 * (LEVELS - 1) + 1 + 2 * QUAD + 1
POOL_B = 2
POOL1 = 6 + LEVELS - 1


def constants():
    import numpy as np
    ident = np.eye(P, dtype=np.float32)
    i = (np.arange(P) % WIN)[:, None]
    j = np.arange(KEYS)[None, :]
    hide = (i < j - WIN) | (i > j)
    mask = np.zeros((P, 2, 2, NWIN, KEYS), np.float32)
    mask[:, :, :, :, :] = np.where(hide, np.float32(-1e30), np.float32(0))[:, None, None, None, :]
    mask[:, 1, :, 0, :WIN] = -1e30
    half = np.arange(0, HD, 2, dtype=np.float64)
    inv_freq = (1.0 / np.float32(10000.0) ** (half.astype(np.float32) / np.float32(HD))).astype(np.float32)
    t = np.arange(TOKENS, dtype=np.float32)
    freqs = (t[:, None] * inv_freq[None, :]).astype(np.float64)
    base = (half + 0.4 * HD) / (1.4 * HD)
    power = ((np.arange(TOKENS) % P) - P // 2)[:, None] / (WIN // 2)
    scale = base[None, :] ** power
    cos, sin = np.cos(freqs), np.sin(freqs)
    tabs = []
    for sc in (scale, 1.0 / scale):
        tabs.append(np.concatenate([cos * sc, cos * sc], -1))
        tabs.append(np.concatenate([-sin * sc, sin * sc], -1))
    rope = np.stack(tabs, 1).astype(np.float32)
    rope = np.ascontiguousarray(rope.reshape(TILES, P, 4 * HD).transpose(1, 0, 2))
    kfac = np.tile(np.concatenate([base, base]) ** (P // (WIN // 2)), 2).astype(np.float32)[:, None]
    r, c = np.arange(P)[:, None], np.arange(P)[None, :]
    lev = []
    for n in range(LEVELS):
        b = 2 ** n
        lev.append(((r // (2 * b)) == (c // (2 * b))) & ((r // b) % 2 == 1) & ((c // b) % 2 == 0))
    lev.append(lev[0].T)
    level = np.ascontiguousarray(np.stack(lev, 1).astype(np.float32))
    return ident, np.ascontiguousarray(mask.reshape(P, 2, 512)), rope, kfac, level


def kernel(L0_attn_x, L0_attn_W0, L0_attn_Wkv, L0_attn_bkv, L0_attn_eta, L0_ffn_Wqkv, L0_ffn_q_scale,
           L0_ffn_k_scale, L0_ffn_Wo, L0_ffn_ln_g, L0_ffn_ln_b, L0_ffn_W1, L0_ffn_b1, L0_ffn_W2, L0_ffn_b2):
    import numpy as np
    import concourse.bacc as bacc
    from concourse.bass_utils import run_bass_kernel_spmd

    ident, mask, rope, kfac, level = constants()
    f = lambda a: np.ascontiguousarray(np.asarray(a))
    wqkv, qs, ks = f(L0_ffn_Wqkv), f(L0_ffn_q_scale), f(L0_ffn_k_scale)
    swap = lambda a: np.concatenate([a[:, HD // 2:], a[:, :HD // 2]], 1)
    inner = HEADS * HD
    par = np.zeros((LAYERS, P, 9), np.float32)
    par[:, :, 0], par[:, :, 1], par[:, :, 8] = f(L0_ffn_ln_g), f(L0_ffn_ln_b), f(L0_ffn_b2)
    b1 = f(L0_ffn_b1)
    for k, (h0, n) in enumerate(HBLK):
        par[:, :n, 2 + k] = b1[:, h0:h0 + n]
        par[:, :n, 5 + k] = b1[:, HID + h0:HID + h0 + n]
    arrays = {
        "x": f(L0_attn_x)[0],
        "wvT": f(f(L0_attn_Wkv)[P:, :].T),
        "w0T": f(f(L0_attn_W0).T),
        "bv": f(L0_attn_bkv)[P:],
        "eta": f(L0_attn_eta).reshape(1),
        "wqk": f(wqkv[:, :, :2 * inner]),
        "scales": f(np.stack([qs, swap(qs), ks, swap(ks)], 1).reshape(LAYERS, 4 * HD)),
        "mvT": f(wqkv[:, :, 2 * inner:].transpose(0, 2, 1).reshape(LAYERS, PAIRS, P, P).transpose(0, 2, 1, 3)),
        "wo": f(L0_ffn_Wo),
        "w1": f(L0_ffn_W1),
        "w2": f(L0_ffn_W2),
        "par": par,
        "ident": ident, "mask": mask, "rope": rope, "kfac": kfac, "level": level,
    }
    nc = bacc.Bacc("TRN2", target_bir_lowering=False, num_devices=1)
    ins = [nc.dram_tensor(f"in_{n}", a.shape, F32, kind="ExternalInput").ap() for n, a in arrays.items()]
    out = nc.dram_tensor("out", (TOKENS, P), F32, kind="ExternalOutput").ap()
    build(nc, *ins, out)
    res = run_bass_kernel_spmd(nc, [{f"in_{n}": a for n, a in arrays.items()}], core_ids=[0])
    return res.results[0]["out"].reshape(1, TOKENS, P)
```
